# Optimizing a Trainium2 kernel written in Bass

```python
import numpy as np
import jax
import jax.numpy as jnp

def _softmax(x, axis=-1):
    return jax.nn.softmax(x, axis=axis)

def _gelu(x):
    return jax.nn.gelu(x, approximate=True)

def _silu(x):
    return jax.nn.silu(x)

def _sigmoid(x):
    return jax.nn.sigmoid(x)

def _layernorm(x, axis=-1, eps=1e-05):
    m = jnp.mean(x, axis=axis, keepdims=True)
    v = jnp.var(x, axis=axis, keepdims=True)
    return (x - m) / jnp.sqrt(v + eps)

def _scatter_add(tgt, idx, src, axis=0):
    return tgt.at[idx].add(src)

def _segment_sum(src, seg, n):
    return jax.ops.segment_sum(src, seg, n)
kernel_name = 'mk_prb_d1_jaxref_r8_adcb2f'

def setup_inputs(seed: int=0):
    np.random.seed(seed)
    _w = jnp.asarray

    def _L0_attn_setup():
        import jax, jax.numpy as jnp
        import numpy as np
        NUM_HEAD = 16
        D_Q = 64
        D_KV = 64
        ROPE_BASE = 10000.0

        def _cos_sin(seq_len, dim):
            pos = jnp.arange(seq_len, dtype=jnp.float32)[:, None]
            ids = jnp.arange(dim // 2, dtype=jnp.float32)
            theta = ROPE_BASE ** (-2.0 * ids) / (dim // 2)
            r = pos * theta[None, :]
            return (jnp.cos(r), jnp.sin(r))

        def _rope(x, cos, sin):
            b, s, d = x.shape
            xv = x.reshape(b, s, d // 2, 2)
            x0, x1 = (xv[..., 0], xv[..., 1])
            out = jnp.stack([x0 * cos - x1 * sin, x1 * cos + x0 * sin], axis=-1)
            return out.reshape(b, s, d)
        key = jax.random.key(seed)
        ks = jax.random.split(key, 10)
        d_model, d_q, d_kv = (128, D_Q, D_KV)
        b, s = (2, 256)
        w = lambda k, i, o: jax.random.normal(k, (i, o), dtype=jnp.float32) * 0.02
        return {'x': jax.random.normal(ks[0], (b, s, d_model), dtype=jnp.float32), 'Wd_q_w': w(ks[1], d_model, d_q), 'Wd_q_b': jnp.zeros((d_q,), jnp.float32), 'Wu_q_w': w(ks[2], d_q, d_model), 'Wu_q_b': jnp.zeros((d_model,), jnp.float32), 'Wq_r_w': w(ks[3], d_q, d_model), 'Wq_r_b': jnp.zeros((d_model,), jnp.float32), 'Wk_r_w': w(ks[4], d_model, d_model), 'Wk_r_b': jnp.zeros((d_model,), jnp.float32), 'Wd_kv_w': w(ks[5], d_model, d_kv), 'Wd_kv_b': jnp.zeros((d_kv,), jnp.float32), 'Wu_k_w': w(ks[6], d_kv, d_model), 'Wu_k_b': jnp.zeros((d_model,), jnp.float32), 'Wu_v_w': w(ks[7], d_kv, d_model), 'Wu_v_b': jnp.zeros((d_model,), jnp.float32), 'Wo_w': w(ks[8], d_model, d_model), 'Wo_b': jnp.zeros((d_model,), jnp.float32)}
    _L0_attn_in = _L0_attn_setup()

    def _L0_ffn_setup():
        import jax, jax.numpy as jnp
        import numpy as np
        DIM = 128

        def _reference_tuple_inner(x, W_r, W_k, W_v, mu_r, mu_k):
            B, T, C = x.shape
            x_prev = jnp.concatenate([jnp.zeros((B, 1, C), x.dtype), x[:, :-1, :]], axis=1)
            xr = mu_r * x + (1.0 - mu_r) * x_prev
            xk = mu_k * x + (1.0 - mu_k) * x_prev
            r = jax.nn.sigmoid(jnp.einsum('btc,dc->btd', xr, W_r))
            k = jnp.einsum('btc,dc->btd', xk, W_k)
            k_act = jnp.square(jax.nn.relu(k))
            out = r * jnp.einsum('btc,dc->btd', k_act, W_v)
            new_state = x[:, -1, :]
            return (out, new_state)
        key = jax.random.key(seed)
        ks = jax.random.split(key, 6)
        B, T, C = (8, 256, DIM)
        x = jax.random.normal(ks[0], (B, T, C), dtype=jnp.float32)
        s = 1.0 / np.sqrt(C)
        W_r = jax.random.uniform(ks[1], (C, C), jnp.float32, -s, s)
        W_k = jax.random.uniform(ks[2], (C, C), jnp.float32, -s, s)
        W_v = jax.random.uniform(ks[3], (C, C), jnp.float32, -s, s)
        mu_r = jax.random.uniform(ks[4], (C,), jnp.float32)
        mu_k = jax.random.uniform(ks[5], (C,), jnp.float32)
        return {'x': x, 'W_r': W_r, 'W_k': W_k, 'W_v': W_v, 'mu_r': mu_r, 'mu_k': mu_k}
    _L0_ffn_in = _L0_ffn_setup()
    _d = {'L0_attn_x': _L0_attn_in['x'], 'L0_attn_Wd_q_w': _L0_attn_in['Wd_q_w'], 'L0_attn_Wd_q_b': _L0_attn_in['Wd_q_b'], 'L0_attn_Wu_q_w': _L0_attn_in['Wu_q_w'], 'L0_attn_Wu_q_b': _L0_attn_in['Wu_q_b'], 'L0_attn_Wq_r_w': _L0_attn_in['Wq_r_w'], 'L0_attn_Wq_r_b': _L0_attn_in['Wq_r_b'], 'L0_attn_Wk_r_w': _L0_attn_in['Wk_r_w'], 'L0_attn_Wk_r_b': _L0_attn_in['Wk_r_b'], 'L0_attn_Wd_kv_w': _L0_attn_in['Wd_kv_w'], 'L0_attn_Wd_kv_b': _L0_attn_in['Wd_kv_b'], 'L0_attn_Wu_k_w': _L0_attn_in['Wu_k_w'], 'L0_attn_Wu_k_b': _L0_attn_in['Wu_k_b'], 'L0_attn_Wu_v_w': _L0_attn_in['Wu_v_w'], 'L0_attn_Wu_v_b': _L0_attn_in['Wu_v_b'], 'L0_attn_Wo_w': _L0_attn_in['Wo_w'], 'L0_attn_Wo_b': _L0_attn_in['Wo_b'], 'L0_ffn_W_r': _L0_ffn_in['W_r'], 'L0_ffn_W_k': _L0_ffn_in['W_k'], 'L0_ffn_W_v': _L0_ffn_in['W_v'], 'L0_ffn_mu_r': _L0_ffn_in['mu_r'], 'L0_ffn_mu_k': _L0_ffn_in['mu_k']}
    _x0 = _d['L0_attn_x']
    _d['L0_attn_x'] = jax.random.normal(jax.random.fold_in(jax.random.key(seed), 1), (8, 512, 128), dtype=_x0.dtype)
    del _x0
    return _d

def reference(L0_attn_x, L0_attn_Wd_q_w, L0_attn_Wd_q_b, L0_attn_Wu_q_w, L0_attn_Wu_q_b, L0_attn_Wq_r_w, L0_attn_Wq_r_b, L0_attn_Wk_r_w, L0_attn_Wk_r_b, L0_attn_Wd_kv_w, L0_attn_Wd_kv_b, L0_attn_Wu_k_w, L0_attn_Wu_k_b, L0_attn_Wu_v_w, L0_attn_Wu_v_b, L0_attn_Wo_w, L0_attn_Wo_b, L0_ffn_W_r, L0_ffn_W_k, L0_ffn_W_v, L0_ffn_mu_r, L0_ffn_mu_k):

    def _L0_attn_ref(x, Wd_q_w, Wd_q_b, Wu_q_w, Wu_q_b, Wq_r_w, Wq_r_b, Wk_r_w, Wk_r_b, Wd_kv_w, Wd_kv_b, Wu_k_w, Wu_k_b, Wu_v_w, Wu_v_b, Wo_w, Wo_b):
        import jax, jax.numpy as jnp
        import numpy as np
        NUM_HEAD = 16
        D_Q = 64
        D_KV = 64
        ROPE_BASE = 10000.0

        def _cos_sin(seq_len, dim):
            pos = jnp.arange(seq_len, dtype=jnp.float32)[:, None]
            ids = jnp.arange(dim // 2, dtype=jnp.float32)
            theta = ROPE_BASE ** (-2.0 * ids) / (dim // 2)
            r = pos * theta[None, :]
            return (jnp.cos(r), jnp.sin(r))

        def _rope(x, cos, sin):
            b, s, d = x.shape
            xv = x.reshape(b, s, d // 2, 2)
            x0, x1 = (xv[..., 0], xv[..., 1])
            out = jnp.stack([x0 * cos - x1 * sin, x1 * cos + x0 * sin], axis=-1)
            return out.reshape(b, s, d)
        b, s, d_model = x.shape
        h = NUM_HEAD
        hd = d_model // h
        scale = jnp.sqrt(jnp.float32(h + D_KV + D_Q))

        def heads(t):
            return t.reshape(b, s, h, hd).transpose(0, 2, 1, 3)
        cos, sin = _cos_sin(s, d_model)
        ct_q = x @ Wd_q_w + Wd_q_b
        qt_c = heads(ct_q @ Wu_q_w + Wu_q_b)
        qt_r = heads(_rope(ct_q @ Wq_r_w + Wq_r_b, cos, sin))
        query = qt_c + qt_r
        ct_kv = x @ Wd_kv_w + Wd_kv_b
        kt_c = heads(ct_kv @ Wu_k_w + Wu_k_b)
        kt_r = heads(_rope(x @ Wk_r_w + Wk_r_b, cos, sin))
        key = kt_c + kt_r
        value = heads(ct_kv @ Wu_v_w + Wu_v_b)
        attn = jnp.einsum('bhqd,bhkd->bhqk', query, key) / scale
        attn = jax.nn.softmax(attn, axis=-1)
        out = jnp.einsum('bhqk,bhkd->bhqd', attn, value)
        out = out.transpose(0, 2, 1, 3).reshape(b, s, d_model)
        return out @ Wo_w + Wo_b

    def _L0_ffn_ref(x, W_r, W_k, W_v, mu_r, mu_k):
        import jax, jax.numpy as jnp
        import numpy as np
        DIM = 128

        def _reference_tuple_inner(x, W_r, W_k, W_v, mu_r, mu_k):
            B, T, C = x.shape
            x_prev = jnp.concatenate([jnp.zeros((B, 1, C), x.dtype), x[:, :-1, :]], axis=1)
            xr = mu_r * x + (1.0 - mu_r) * x_prev
            xk = mu_k * x + (1.0 - mu_k) * x_prev
            r = jax.nn.sigmoid(jnp.einsum('btc,dc->btd', xr, W_r))
            k = jnp.einsum('btc,dc->btd', xk, W_k)
            k_act = jnp.square(jax.nn.relu(k))
            out = r * jnp.einsum('btc,dc->btd', k_act, W_v)
            new_state = x[:, -1, :]
            return (out, new_state)
        return _reference_tuple_inner(x, W_r, W_k, W_v, mu_r, mu_k)[0]
    x = L0_attn_x
    xn = _layernorm(x, axis=-1)
    x = x + _L0_attn_ref(xn, L0_attn_Wd_q_w, L0_attn_Wd_q_b, L0_attn_Wu_q_w, L0_attn_Wu_q_b, L0_attn_Wq_r_w, L0_attn_Wq_r_b, L0_attn_Wk_r_w, L0_attn_Wk_r_b, L0_attn_Wd_kv_w, L0_attn_Wd_kv_b, L0_attn_Wu_k_w, L0_attn_Wu_k_b, L0_attn_Wu_v_w, L0_attn_Wu_v_b, L0_attn_Wo_w, L0_attn_Wo_b) + _L0_ffn_ref(xn, L0_ffn_W_r, L0_ffn_W_k, L0_ffn_W_v, L0_ffn_mu_r, L0_ffn_mu_k)
    return x

_drawn_inputs = setup_inputs


def setup_inputs(seed=0):
    import zlib

    import numpy as np

    out = dict(_drawn_inputs(seed))
    spreads = {'L0_attn_Wd_q_b': (0.0, 0.8),
     'L0_attn_Wu_q_b': (0.0, 0.8),
     'L0_attn_Wq_r_b': (0.0, 0.8),
     'L0_attn_Wk_r_b': (0.0, 0.8),
     'L0_attn_Wd_kv_b': (0.0, 0.8),
     'L0_attn_Wu_k_b': (0.0, 0.8),
     'L0_attn_Wu_v_b': (0.0, 0.369),
     'L0_attn_Wo_b': (0.0, 0.1)}
    factors = {'L0_attn_Wd_q_w': 8.0,
     'L0_attn_Wu_q_w': 8.0,
     'L0_attn_Wq_r_w': 8.0,
     'L0_attn_Wk_r_w': 8.0,
     'L0_attn_Wd_kv_w': 8.0,
     'L0_attn_Wu_k_w': 8.0,
     'L0_attn_Wu_v_w': 8.0,
     'L0_attn_Wo_w': 2.685,
     'L0_ffn_W_r': 3.169,
     'L0_ffn_mu_r': 6.232}
    for name, (base, spread) in spreads.items():
        noise = np.random.default_rng([zlib.crc32(name.encode()), seed]).standard_normal(out[name].shape)
        drawn = base * np.exp(spread * noise) if base else spread * noise
        out[name] = jnp.asarray(drawn.astype(out[name].dtype))
    for name, factor in factors.items():
        out[name] = (out[name] * factor).astype(out[name].dtype)
    return out
```

```python
from contextlib import ExitStack

import concourse.bass as bass
from concourse import mybir

F32 = mybir.dt.float32
BF16 = mybir.dt.bfloat16
ACT = mybir.ActivationFunctionType
ALU = mybir.AluOpType
AX_X = mybir.AxisListType.X

P = 128
B, S, D = 8, 512, 128
H = 16
HD = D // H
DL = 64
T = S // P
UNITS = 4
HPU = H // UNITS
STEPS = 8
SPB = UNITS * STEPS
LEAD = 12
PAIRS = H // 2
GROUP = 64
RUNS = ((0, 3), (1, 2), (2, 1))
PRODUCTS = sum(n for _, n in RUNS)
ROWS = PRODUCTS * HD
ROWS_MAX = ROWS + 3
VW = 32
EPS = 1e-5
SCALE = 1.0 / float(H + DL + DL) ** 0.5
DMA = 16

DOWN, KROPE, KROPE_ROT, OUT, FFN_R, FFN_K, FFN_V, IDENT = range(8)
UP, QROPE, QROPE_ROT = range(3)
UP_V = 1
B_DOWN, B_UQ, B_QR, B_QR_ROT, B_UK, B_KR, B_KR_ROT, MU_R, MU_K, OMU_R, OMU_K = range(11)


STACKS = 2 * len(RUNS)


def head_of(u, j):
    return PAIRS * (j % 2) + 2 * u + j // 2


def build(nc, x, w_sq_dram, w_lat_dram, cols_dram, rows_dram, trig_dram, ident_dram, out):
    x_view = x.rearrange("b (t p) c -> b p t c", p=P)
    out_view = out.rearrange("b (t p) c -> b p t c", p=P)

    with ExitStack() as ctx:
        def sb(name, shape, dt=F32):
            return ctx.enter_context(nc.sbuf_tensor(name, shape, dt))

        def psum(name, shape, dt=F32):
            return ctx.enter_context(nc.psum_tensor(name, shape, dt))

        def sem(name):
            return ctx.enter_context(nc.semaphore(name))

        w_sq = sb("w_sq", [P, 8, P])
        w_lat = sb("w_lat", [P, 3, P])
        cols = sb("cols", [P, 11])
        rows = sb("rows", [P, 2, P])
        trig = sb("trig", [P, 2, S])
        ident_bf = sb("ident_bf", [P, P], BF16)
        half = sb("half", [P, T])
        x_in = [sb(f"x_in{i}", [P, T, D]) for i in range(2)]
        stats = sb("stats", [P, T, 6])
        mean_var = sb("mean_var", [P, T, 2])
        var_eps = sb("var_eps", [P, T])
        rstd = sb("rstd", [P, T])
        xn = sb("xn", [P, T, D])
        xT = sb("xT", [P, 1 + S])
        latT = sb("latT", [P, S])
        rot_c = {n: sb(f"{n}_rot_c", [P, S]) for n in "qk"}
        rot_s = {n: sb(f"{n}_rot_s", [P, S]) for n in "qk"}
        rot = {n: sb(f"{n}_rot", [P, S]) for n in "qk"}
        full = {n: sb(f"{n}_full", [P, S]) for n in "qk"}
        rest = {n: sb(f"{n}_rest", [P, S]) for n in "qk"}
        parts = {n: sb(f"{n}_parts", [P, 3, S], BF16) for n in "qk"}
        q_stack = [sb(f"q_stack{i}", [P, PAIRS, S], BF16) for i in range(2)]
        k_stack = [sb(f"k_stack{i}", [P, PAIRS, S], BF16) for i in range(2)]
        vals = [sb(f"vals{i}", [P, T, H, VW]) for i in range(2)]
        probs = sb("probs", [P, STEPS, 2, S])
        neg_max = [sb(f"neg_max{i}", [P, 2, 8]) for i in range(2)]
        max_rest = sb("max_rest", [P, 2, 8])
        max_cols = sb("max_cols", [P, P], BF16)
        max_parts = max_cols[:, 0:48].rearrange("p (g k c) -> p g k c", g=2, k=3)
        zeros = sb("zeros", [P, 2, 8])
        max_rows = [sb(f"max_rows{i}", [48, P], BF16) for i in range(2)]
        pv = [sb(f"pv{i}", [P, S]) for i in range(2)]
        num = sb("num", [P, S])
        den = sb("den", [P, S])
        rden = sb("rden", [P, S])
        attnT = sb("attnT", [P, S])
        mix_a = {n: sb(f"mix_a_{n}", [P, S]) for n in "rk"}
        mix_b = {n: sb(f"mix_b_{n}", [P, S]) for n in "rk"}
        mixed = {n: sb(f"mixed_{n}", [P, S]) for n in "rk"}
        gate = sb("gate", [P, T, D])
        relu = sb("relu", [P, S])
        relu_sq = sb("relu_sq", [P, S])
        gated = sb("gated", [P, T, D])
        x_bias = sb("x_bias", [P, T, D])
        base = [sb(f"base{i}", [P, T, D]) for i in range(2)]
        y = sb("y", [P, T, D])

        ps_max = [psum(f"ps_max{g}", [P, S]) for g in range(2)]
        ps_exp = [psum(f"ps_exp{i}", [P, 2, S]) for i in range(2)]
        ps_pv = psum("ps_pv", [P, S])
        ps_misc = psum("ps_misc", [P, S])
        ps_misc_bf = ps_misc[:, :].bitcast(BF16)
        ps_tok = ps_misc[:, :].rearrange("p (t c) -> p t c", t=T)

        spills = {n: nc.dram_tensor(f"{n}_spill", (3, HD, H, S), BF16, kind="Internal").ap() for n in "qk"}

        consts_in = sem("consts_in")
        fills = sem("fills")
        fills_dve = sem("fills_dve")
        omu_ready = sem("omu_ready")
        x_landed = sem("x_landed")
        stats_ready = sem("stats_ready")
        mv_ready = sem("mv_ready")
        var_ready = sem("var_ready")
        rstd_ready = sem("rstd_ready")
        xn_ready = sem("xn_ready")
        JOBS = ("xT", "k_cos", "k_sin", "lat", "k_lin", "q_cos", "q_sin", "q_lin", "vals",
                "ffn_r", "ffn_k", "ffn_v", "out", "max")
        ready = {n: sem(f"{n}_ready") for n in JOBS}
        taken = {n: sem(f"{n}_taken") for n in JOBS}
        rot_ready = {n: sem(f"{n}_rot_ready") for n in "qk"}
        part0_ready = {n: sem(f"{n}_part0_ready") for n in "qk"}
        rest_ready = {n: sem(f"{n}_rest_ready") for n in "qk"}
        part1_ready = {n: sem(f"{n}_part1_ready") for n in "qk"}
        part2_ready = {n: sem(f"{n}_part2_ready") for n in "qk"}
        spilled = {n: sem(f"{n}_spilled") for n in "qk"}
        stacked = {n: sem(f"{n}_stacked") for n in "qk"}
        mix_half = sem("mix_half")
        mixed_ready = {n: sem(f"mixed_{n}_ready") for n in "rk"}
        relu_sq_ready = sem("relu_sq_ready")
        x_bias_ready = sem("x_bias_ready")
        base_ready = sem("base_ready")
        raw_scores = [sem(f"raw_scores{g}") for g in range(2)]
        row_max = [sem(f"row_max{g}") for g in range(2)]
        max_split = sem("max_split")
        max_parts_ready = sem("max_parts_ready")
        max_stacked = [sem(f"max_stacked{i}") for i in range(2)]
        scores_ready = sem("scores_ready")
        probs_ready = sem("probs_ready")
        pv_done = sem("pv_done")
        pv_taken = sem("pv_taken")
        pv_gathered = [sem(f"pv_gathered{i}") for i in range(2)]
        rden_ready = sem("rden_ready")
        attn_ready = sem("attn_ready")
        stored = sem("stored")

        block = ctx.enter_context(nc.Block())


        def batches(eng, body):
            body(0, 0)
            with eng.Fori(0, (B - 2) // 2) as i:
                body(2 * i + 1, 1)
                body(2 * i + 2, 0)
            body(B - 1, 1)

        def first(b):
            return isinstance(b, int) and b == 0

        def last(b):
            return isinstance(b, int) and b == B - 1

        @block.sync
        def _(sp):
            def value(count):
                if not isinstance(count, int):
                    sp.compute_val(count)
                return count

            def load_x(n, par):
                sp.dma_start(x_in[par][:, :, :], x_view[n]).then_inc(x_landed, DMA)

            def spill(name, n):
                copies_read = value(STACKS * DMA * n)
                sp.wait_ge(part2_ready[name], n + 1)
                if not (isinstance(n, int) and n == 0):
                    sp.wait_ge(stacked[name], copies_read)
                for part in range(3):
                    sp.dma_start(spills[name][part].rearrange("d h q -> h d q"),
                                 parts[name][:, part, :]).then_inc(spilled[name], DMA)

            def stack(name, n, par):
                scores_read = value(SPB * (n - 1))
                sp.wait_ge(spilled[name], 3 * DMA * (n + 1))
                if not (isinstance(n, int) and n < 2):
                    sp.wait_ge(scores_ready, scores_read)
                dst = (q_stack if name == "q" else k_stack)[par]
                for g in range(2):
                    at = GROUP * g
                    for q_part, count in RUNS:
                        heads = spills[name][:, :, PAIRS * g:PAIRS * (g + 1), :]
                        if name == "q":
                            src = heads[q_part:q_part + 1].to_broadcast([count, HD, PAIRS, S])
                        else:
                            src = heads[0:count]
                        sp.dma_start(dst[at:at + HD * count, :, :], src).then_inc(stacked[name], DMA)
                        at += HD * count

            def stack_max(unit, u, par, x_read=None):
                sp.wait_ge(taken["max"], unit + 1)
                if x_read is not None:
                    sp.wait_ge(x_bias_ready, x_read)
                for g in range(2):
                    at = GROUP * g + ROWS
                    sp.dma_start(q_stack[par][at:at + 3, 2 * u:2 * u + 2, :],
                                 max_rows[u % 2][24 * g:24 * g + 24, :]).then_inc(max_stacked[u % 2], DMA)

            def gather(unit, u, b):
                sp.wait_ge(pv_taken, unit + 1)
                if u == 0 and not first(b):
                    sp.wait_ge(attn_ready, b)
                for j in range(HPU):
                    at, r = HD * head_of(u, j), VW * j
                    sp.dma_start(num[at:at + HD, :], pv[u % 2][r:r + HD, :]).then_inc(pv_gathered[u % 2], DMA)
                    sp.dma_start(den[at:at + HD, :], pv[u % 2][r + HD:r + 2 * HD, :]).then_inc(pv_gathered[u % 2], DMA)

            def store(b):
                sp.wait_ge(taken["out"], b + 1)
                sp.dma_start(out_view[b], y[:, :, :]).then_inc(stored, DMA)

            def body(b, par):
                for s in range(SPB):
                    u = s // STEPS
                    if s == 0 and not last(b):
                        load_x(b + 1, 1 - par)
                    if s % STEPS == 3 and not (u == 0 and first(b)):
                        v = (u - 1) % UNITS
                        gather(UNITS * b + u - 1, v, b if u else b - 1)
                    if s % STEPS == 6:
                        nxt = u + 1
                        if nxt < UNITS:
                            stack_max(UNITS * b + nxt, nxt, par)
                        elif not last(b):
                            stack_max(UNITS * b + nxt, 0, 1 - par, x_read=b + 1)
                    if not last(b):
                        if s == 12:
                            spill("k", b + 1)
                        if s == 13:
                            stack("k", b + 1, 1 - par)
                        if s == 15:
                            spill("q", b + 1)
                        if s == 16:
                            stack("q", b + 1, 1 - par)
                    if s == 17 and not first(b):
                        store(b - 1)

            sp.dma_start(x_in[0][:, :, :], x_view[0]).then_inc(x_landed, DMA)
            sp.dma_start(w_sq[:, :, :], w_sq_dram).then_inc(consts_in, DMA)
            sp.dma_start(cols[:, 0:9], cols_dram).then_inc(consts_in, DMA)
            sp.dma_start(trig[:, :, :], trig_dram).then_inc(consts_in, DMA)
            sp.dma_start(w_lat[:, :, :], w_lat_dram).then_inc(consts_in, DMA)
            sp.dma_start(rows[:, :, :], rows_dram).then_inc(consts_in, DMA)
            sp.dma_start(ident_bf[:, :], ident_dram).then_inc(consts_in, DMA)
            sp.wait_ge(fills, 3)
            for name in "kq":
                spill(name, 0)
                stack(name, 0, 0)
            stack_max(0, 0, 0)
            batches(sp, body)
            gather(UNITS * B - 1, UNITS - 1, B - 1)
            store(B - 1)
            sp.wait_ge(stored, DMA * B)

        CONSTS = 6 * DMA

        @block.tensor
        def _(pe):
            mm = nc.tensor.matmul

            def project(job, w, rhs):
                mm(ps_misc[:, :], w, rhs, start=True, stop=True).then_inc(ready[job], 1)

            def transpose_x(n):
                pe.wait_ge(xn_ready, n + 1)
                if not (isinstance(n, int) and n == 0):
                    pe.wait_ge(taken["max"], UNITS * (n - 1) + 2)
                for t in range(T):
                    last_mm = nc.tensor.transpose(ps_tok[:, t, :], xn[:, t, :], w_sq[:, IDENT, :])
                last_mm.then_inc(ready["xT"], 1)

            def k_cos(n):
                pe.wait_ge(taken["xT"], n + 1)
                project("k_cos", w_sq[:, KROPE, :], xT[:, 1:1 + S])

            def k_sin(n):
                pe.wait_ge(taken["k_cos"], n + 1)
                project("k_sin", w_sq[:, KROPE_ROT, :], xT[:, 1:1 + S])

            def latents(n):
                pe.wait_ge(taken["k_sin"], n + 1)
                project("lat", w_sq[:, DOWN, :], xT[:, 1:1 + S])

            def k_lin(n):
                pe.wait_ge(taken["lat"], n + 1)
                project("k_lin", w_lat[DL:P, UP, :], latT[DL:P, :])

            def q_cos(n):
                pe.wait_ge(taken["k_lin"], n + 1)
                project("q_cos", w_lat[0:DL, QROPE, :], latT[0:DL, :])

            def q_sin(n):
                pe.wait_ge(taken["q_cos"], n + 1)
                project("q_sin", w_lat[0:DL, QROPE_ROT, :], latT[0:DL, :])

            def q_lin(n):
                pe.wait_ge(taken["q_sin"], n + 1)
                project("q_lin", w_lat[0:DL, UP, :], latT[0:DL, :])

            def values(n):
                pe.wait_ge(taken["q_lin"], n + 1)
                for t in range(T):
                    last_mm = mm(ps_tok[:, t, :], latT[DL:P, t * P:(t + 1) * P], w_lat[DL:P, UP_V, :],
                                 start=True, stop=True)
                last_mm.then_inc(ready["vals"], 1)

            def ffn_r(n, before):
                pe.wait_ge(*before)
                pe.wait_ge(mixed_ready["r"], n + 1)
                for t in range(T):
                    last_mm = mm(ps_tok[:, t, :], mixed["r"][:, t * P:(t + 1) * P], w_sq[:, FFN_R, :],
                                 start=True, stop=True)
                last_mm.then_inc(ready["ffn_r"], 1)

            def ffn_k(n):
                pe.wait_ge(taken["ffn_r"], n + 1)
                pe.wait_ge(mixed_ready["k"], n + 1)
                project("ffn_k", w_sq[:, FFN_K, :], mixed["k"][:, :])

            def ffn_v(n):
                pe.wait_ge(taken["ffn_k"], n + 1)
                pe.wait_ge(relu_sq_ready, n + 1)
                for t in range(T):
                    last_mm = mm(ps_tok[:, t, :], relu_sq[:, t * P:(t + 1) * P], w_sq[:, FFN_V, :],
                                 start=True, stop=True)
                last_mm.then_inc(ready["ffn_v"], 1)

            def transpose_max(unit, before):
                pe.wait_ge(*before)
                pe.wait_ge(max_parts_ready, unit + 1)
                nc.tensor.transpose(ps_misc_bf[:, 0:P], max_cols[:, :], ident_bf[:, :]).then_inc(ready["max"], 1)

            def out_projection(b, before):
                pe.wait_ge(*before)
                pe.wait_ge(attn_ready, b + 1)
                for t in range(T):
                    last_mm = mm(ps_tok[:, t, :], attnT[:, t * P:(t + 1) * P], w_sq[:, OUT, :],
                                 start=True, stop=True)
                last_mm.then_inc(ready["out"], 1)

            def scores_for_max(b, par, r, g):
                pair, qt = r // T, r % T
                if r == 0 and g == 0:
                    pe.wait_ge(stacked["k"], STACKS * DMA * (b + 1))
                    pe.wait_ge(stacked["q"], STACKS * DMA * (b + 1))
                if not (first(b) and r == 0):
                    pe.wait_ge(row_max[g], SPB * b + r)
                at = slice(GROUP * g, GROUP * g + ROWS)
                mm(ps_max[g][:, :], q_stack[par][at, pair, qt * P:(qt + 1) * P], k_stack[par][at, pair, :],
                   start=True, stop=True).then_inc(raw_scores[g], 1)

            def scores_for_exp(b, par, s):
                u, kt, pp = s // STEPS, s % STEPS // 2, s % 2
                pair = 2 * u + pp
                if s % STEPS == 0:
                    pe.wait_ge(max_stacked[u % 2], 2 * DMA * (UNITS // 2 * b + u // 2 + 1))
                if not (first(b) and s < 2):
                    pe.wait_ge(probs_ready, SPB * b + s - 1)
                for g in range(2):
                    at = slice(GROUP * g, GROUP * g + ROWS_MAX)
                    last_mm = mm(ps_exp[s % 2][:, g, :], k_stack[par][at, pair, kt * P:(kt + 1) * P],
                                 q_stack[par][at, pair, :], start=True, stop=True)
                last_mm.then_inc(scores_ready, 1)

            def probs_values(b, par, u, kt):
                pe.wait_ge(probs_ready, SPB * b + STEPS * u + 2 * kt + 2)
                if kt == 0 and not (first(b) and u == 0):
                    pe.wait_ge(pv_taken, UNITS * b + u)
                for j in range(HPU):
                    last_mm = mm(ps_pv[VW * j:VW * (j + 1), :], vals[par][:, kt, head_of(u, j), :],
                                 probs[:, 2 * kt + j // 2, j % 2, :], start=kt == 0, stop=kt == T - 1)
                last_mm.then_inc(pv_done, 1)

            def ahead(b, par, s, g):
                r = s + LEAD
                if r < SPB:
                    scores_for_max(b, par, r, g)
                elif not last(b):
                    scores_for_max(b + 1, 1 - par, r - SPB, g)

            def body(b, par):
                n, more = b + 1, not last(b)
                for s in range(SPB):
                    u = s // STEPS
                    ahead(b, par, s, 0)
                    scores_for_exp(b, par, s)
                    if s % STEPS in (3, 5, 7):
                        probs_values(b, par, u, (s % STEPS - 3) // 2)
                    elif s % STEPS == 1 and s > 1:
                        probs_values(b, par, u - 1, T - 1)
                    elif s == 1 and not first(b):
                        probs_values(b - 1, 1 - par, UNITS - 1, T - 1)
                    ahead(b, par, s, 1)
                    if s == 5:
                        transpose_max(UNITS * b + 1, (taken["max"], UNITS * b + 1))
                    if more:
                        if s == 5:
                            transpose_x(n)
                        if s == 6:
                            k_cos(n)
                        if s == 7:
                            k_sin(n)
                        if s == 8:
                            latents(n)
                        if s == 9:
                            k_lin(n)
                        if s == 10:
                            q_cos(n)
                        if s == 11:
                            q_sin(n)
                        if s == 12:
                            q_lin(n)
                        if s == 13:
                            values(n)
                    if s == 13:
                        transpose_max(UNITS * b + 2, (taken["vals"], n + 1) if more
                                      else (taken["max"], UNITS * b + 2))
                    if s == 14 and not first(b):
                        out_projection(b - 1, (taken["max"], UNITS * b + 3))
                    if more:
                        if s == 16:
                            ffn_r(n, (taken["max"], UNITS * b + 3) if first(b) else (taken["out"], b))
                        if s == 17:
                            ffn_k(n)
                        if s == 19:
                            ffn_v(n)
                    if s == 21:
                        transpose_max(UNITS * b + 3, (taken["ffn_v"], n + 1) if more
                                      else (taken["out"], b))
                    if s == 29 and more:
                        transpose_max(UNITS * b + 4, (taken["max"], UNITS * b + 4))

            pe.wait_ge(consts_in, CONSTS)
            pe.wait_ge(fills, 3)
            transpose_x(0)
            k_cos(0)
            k_sin(0)
            latents(0)
            k_lin(0)
            q_cos(0)
            q_sin(0)
            q_lin(0)
            values(0)
            ffn_r(0, (taken["vals"], 1))
            ffn_k(0)
            ffn_v(0)
            for r in range(STEPS):
                for g in range(2):
                    scores_for_max(0, 0, r, g)
            transpose_max(0, (taken["ffn_v"], 1))
            for r in range(STEPS, LEAD):
                for g in range(2):
                    scores_for_max(0, 0, r, g)
            batches(pe, body)
            probs_values(B - 1, 1, UNITS - 1, T - 1)
            out_projection(B - 1, (taken["max"], UNITS * B))

        @block.scalar
        def _(act):
            activation = nc.scalar.activation

            def take_xT(n):
                act.wait_ge(ready["xT"], n + 1)
                if not (isinstance(n, int) and n == 0):
                    act.wait_ge(ready["lat"], n)
                    act.wait_ge(mixed_ready["k"], n)
                activation(xT[:, 1:1 + S], ps_misc[:, :], ACT.Copy).then_inc(taken["xT"], 1)

            def take_latents(n):
                act.wait_ge(ready["lat"], n + 1)
                if not (isinstance(n, int) and n == 0):
                    act.wait_ge(ready["vals"], n)
                activation(latT[:, :], ps_misc[:, :], ACT.Identity,
                           bias=cols[:, B_DOWN:B_DOWN + 1]).then_inc(taken["lat"], 1)

            def part0(name, n):
                act.wait_ge(taken[f"{name}_lin"], n + 1)
                if not (isinstance(n, int) and n == 0):
                    act.wait_ge(stacked[name], STACKS * DMA * n)
                activation(parts[name][:, 0, :], full[name][:, :], ACT.Copy).then_inc(part0_ready[name], 1)

            def part1(name, n):
                act.wait_ge(rest_ready[name], n + 1)
                activation(parts[name][:, 1, :], rest[name][:, :], ACT.Copy).then_inc(part1_ready[name], 1)

            def take_max(b, u):
                act.wait_ge(ready["max"], UNITS * b + u + 1)
                if not (first(b) and u < 2):
                    act.wait_ge(max_stacked[u % 2], 2 * DMA * (UNITS // 2 * b + u // 2))
                activation(max_rows[u % 2][:, :], ps_misc_bf[0:48, 0:P], ACT.Copy).then_inc(taken["max"], 1)

            def take_ffn_r(n):
                act.wait_ge(ready["ffn_r"], n + 1)
                if not (isinstance(n, int) and n == 0):
                    act.wait_ge(taken["ffn_v"], n)
                activation(gate[:, :, :], ps_tok, ACT.Tanh, scale=0.5).then_inc(taken["ffn_r"], 1)

            def take_ffn_k(n):
                act.wait_ge(ready["ffn_k"], n + 1)
                if not (isinstance(n, int) and n == 0):
                    act.wait_ge(relu_sq_ready, n)
                activation(relu[:, :], ps_misc[:, :], ACT.Relu).then_inc(taken["ffn_k"], 1)

            def softmax_exp(b, s):
                act.wait_ge(scores_ready, SPB * b + s + 1)
                if not (first(b) and s < STEPS):
                    act.wait_ge(pv_done, T * (UNITS * b + s // STEPS - 1) + s % STEPS // 2 + 1)
                activation(probs[:, s % STEPS, :, :], ps_exp[s % 2][:, :, :], ACT.Exp,
                           scale=SCALE).then_inc(probs_ready, 1)

            def take_pv(b, u):
                act.wait_ge(pv_done, T * (UNITS * b + u + 1))
                if not (first(b) and u < 2):
                    act.wait_ge(pv_gathered[u % 2], 2 * HPU * DMA * (UNITS // 2 * b + u // 2))
                activation(pv[u % 2][:, :], ps_pv[:, :], ACT.Copy).then_inc(pv_taken, 1)

            def body(b, par):
                n, more = b + 1, not last(b)
                for s in range(SPB):
                    u = s // STEPS
                    softmax_exp(b, s)
                    if s % STEPS == 2 and u > 0:
                        take_pv(b, u - 1)
                    elif s == 2 and not first(b):
                        take_pv(b - 1, UNITS - 1)
                    if s % STEPS == 5 and (more or u < UNITS - 1):
                        take_max(b, u + 1)
                    if more:
                        if s == 5:
                            take_xT(n)
                        if s == 8:
                            take_latents(n)
                        if s == 10:
                            part0("k", n)
                        if s == 11:
                            part1("k", n)
                        if s == 13:
                            part0("q", n)
                        if s == 14:
                            part1("q", n)
                        if s == 16:
                            take_ffn_r(n)
                        if s == 17:
                            take_ffn_k(n)

            act.wait_ge(consts_in, CONSTS)
            take_xT(0)
            take_latents(0)
            part0("k", 0)
            part1("k", 0)
            part0("q", 0)
            part1("q", 0)
            take_ffn_r(0)
            take_ffn_k(0)
            take_max(0, 0)
            batches(act, body)
            take_pv(B - 1, UNITS - 1)

        @block.vector
        def _(dve):
            vec = nc.vector

            def layer_norm_stats(n, par):
                dve.wait_ge(x_landed, DMA * (n + 1))
                for t in range(T):
                    last_op = vec.bn_stats(stats[:, t, :], x_in[par][:, t, :])
                last_op.then_inc(stats_ready, 1)

            def mean_variance(n):
                for t in range(T):
                    last_op = vec.bn_aggr(mean_var[:, t, :], stats[:, t, :])
                last_op.then_inc(mv_ready, 1)
                dve.wait_ge(mv_ready, n + 1)
                vec.tensor_scalar(var_eps[:, :], mean_var[:, :, 1], EPS, None, ALU.add).then_inc(var_ready, 1)

            def layer_norm(n, par):
                dve.wait_ge(rstd_ready, n + 1)
                if not (isinstance(n, int) and n == 0):
                    dve.wait_ge(ready["xT"], n)
                for t in range(T):
                    last_op = vec.tensor_scalar(xn[:, t, :], x_in[par][:, t, :], mean_var[:, t, 0:1],
                                                rstd[:, t:t + 1], ALU.subtract, ALU.mult)
                last_op.then_inc(xn_ready, 1)

            def rope_half(name, which, n):
                job = f"{name}_{which}"
                dve.wait_ge(ready[job], n + 1)
                if not (isinstance(n, int) and n == 0):
                    dve.wait_ge(rot_ready[name], n)
                bias = {"q_cos": B_QR, "q_sin": B_QR_ROT, "k_cos": B_KR, "k_sin": B_KR_ROT}[job]
                dst = (rot_c if which == "cos" else rot_s)[name]
                vec.scalar_tensor_tensor(dst[:, :], ps_misc[:, :], cols[:, bias:bias + 1],
                                         trig[:, 0 if which == "cos" else 1, :],
                                         ALU.add, ALU.mult).then_inc(taken[job], 1)

            def add_linear(name, n):
                dve.wait_ge(ready[f"{name}_lin"], n + 1)
                dve.wait_ge(rot_ready[name], n + 1)
                if not (isinstance(n, int) and n == 0):
                    dve.wait_ge(rest_ready[name], n)
                bias = B_UQ if name == "q" else B_UK
                vec.scalar_tensor_tensor(full[name][:, :], ps_misc[:, :], cols[:, bias:bias + 1],
                                         rot[name][:, :], ALU.add, ALU.add).then_inc(taken[f"{name}_lin"], 1)

            def take_values(n, par):
                dve.wait_ge(ready["vals"], n + 1)
                if not (isinstance(n, int) and n < 2):
                    dve.wait_ge(pv_done, T * UNITS * (n - 1))
                for t in range(T):
                    last_op = vec.tensor_tensor(vals[par][:, t, :, 0:HD],
                                                ps_tok[:, t, :].rearrange("p (h d) -> p h d", d=HD),
                                                rows[:, 0, :].rearrange("p (h d) -> p h d", d=HD), ALU.add)
                last_op.then_inc(taken["vals"], 1)

            def take_ffn_v(n):
                dve.wait_ge(ready["ffn_v"], n + 1)
                dve.wait_ge(taken["ffn_r"], n + 1)
                if not (isinstance(n, int) and n == 0):
                    dve.wait_ge(base_ready, n)
                vec.scalar_tensor_tensor(gated[:, :, :], gate[:, :, :], 1.0, ps_tok,
                                         ALU.add, ALU.mult).then_inc(taken["ffn_v"], 1)

            def normalise(b):
                for gathered in pv_gathered:
                    dve.wait_ge(gathered, HPU * DMA * UNITS * (b + 1))
                vec.reciprocal(rden[:, :], den[:, :]).then_inc(rden_ready, 1)
                dve.wait_ge(rden_ready, b + 1)
                if not first(b):
                    dve.wait_ge(ready["out"], b)
                vec.tensor_tensor(attnT[:, :], num[:, :], rden[:, :], ALU.mult).then_inc(attn_ready, 1)

            def finish(b, par):
                dve.wait_ge(ready["out"], b + 1)
                dve.wait_ge(base_ready, b + 1)
                if not first(b):
                    dve.wait_ge(stored, DMA * b)
                vec.tensor_tensor(y[:, :, :], ps_tok, base[par][:, :, :], ALU.add).then_inc(taken["out"], 1)

            def reduce_rows(b, r, g):
                unit, c = r // STEPS, r % STEPS
                dve.wait_ge(raw_scores[g], SPB * b + r + 1)
                if c == 0 and g == 0 and not (first(b) and unit < 2):
                    dve.wait_ge(max_parts_ready, UNITS * b + unit - 1)
                vec.tensor_reduce(neg_max[unit % 2][:, g, c:c + 1], ps_max[g][:, :], AX_X, ALU.max,
                                  negate=True).then_inc(row_max[g], 1)

            def ahead(b, s, g):
                r = s + LEAD
                if r < SPB:
                    reduce_rows(b, r, g)
                elif not last(b):
                    reduce_rows(b + 1, r - SPB, g)

            def body(b, par):
                n, more = b + 1, not last(b)
                for s in range(SPB):
                    ahead(b, s, 0)
                    if more and s == 3:
                        dve.wait_ge(stats_ready, n + 1)
                    ahead(b, s, 1)
                    if more:
                        if s == 2:
                            layer_norm_stats(n, 1 - par)
                        if s == 3:
                            mean_variance(n)
                        if s == 4:
                            layer_norm(n, 1 - par)
                        if s == 6:
                            rope_half("k", "cos", n)
                        if s == 7:
                            rope_half("k", "sin", n)
                    if s == 8 and not first(b):
                        normalise(b - 1)
                    if more:
                        if s == 9:
                            add_linear("k", n)
                        if s == 10:
                            rope_half("q", "cos", n)
                        if s == 11:
                            rope_half("q", "sin", n)
                        if s == 12:
                            add_linear("q", n)
                        if s == 13:
                            take_values(n, 1 - par)
                    if s == 14 and not first(b):
                        finish(b - 1, 1 - par)
                    if s == 19 and more:
                        take_ffn_v(n)

            for buf in vals:
                vec.memset(buf[:, :, :, :], 1.0)
            vec.memset(half[:, :], -0.5)
            vec.memset(xT[:, 0:1], 0.0).then_inc(fills, 1)
            dve.wait_ge(consts_in, CONSTS)
            vec.tensor_scalar(cols[:, OMU_R:OMU_K + 1], cols[:, MU_R:MU_K + 1], -1.0, 1.0,
                              ALU.mult, ALU.add).then_inc(omu_ready, 1)
            vec.tensor_scalar(w_sq[:, FFN_V, :], w_sq[:, FFN_V, :], 0.5, None, ALU.mult).then_inc(fills, 1)
            layer_norm_stats(0, 0)
            dve.wait_ge(stats_ready, 1)
            mean_variance(0)
            layer_norm(0, 0)
            rope_half("k", "cos", 0)
            rope_half("k", "sin", 0)
            add_linear("k", 0)
            rope_half("q", "cos", 0)
            rope_half("q", "sin", 0)
            add_linear("q", 0)
            take_values(0, 0)
            take_ffn_v(0)
            for r in range(LEAD):
                for g in range(2):
                    reduce_rows(0, r, g)
            batches(dve, body)
            normalise(B - 1)
            finish(B - 1, 1)

        @block.gpsimd
        def _(pool):
            gp = nc.gpsimd

            def inverse_std(n):
                pool.wait_ge(var_ready, n + 1)
                gp.tensor_tensor(rstd[:, :], var_eps[:, :], half[:, :], ALU.pow).then_inc(rstd_ready, 1)

            def add_halves(name, n):
                pool.wait_ge(taken[f"{name}_sin"], n + 1)
                if not (isinstance(n, int) and n == 0):
                    pool.wait_ge(taken[f"{name}_lin"], n)
                gp.tensor_tensor(rot[name][:, :], rot_c[name][:, :], rot_s[name][:, :],
                                 ALU.add).then_inc(rot_ready[name], 1)

            def rest_after_part0(name, n):
                pool.wait_ge(part0_ready[name], n + 1)
                gp.tensor_tensor(rest[name][:, :], full[name][:, :], parts[name][:, 0, :],
                                 ALU.subtract).then_inc(rest_ready[name], 1)

            def part2(name, n):
                pool.wait_ge(part1_ready[name], n + 1)
                gp.tensor_tensor(parts[name][:, 2, :], rest[name][:, :], parts[name][:, 1, :],
                                 ALU.subtract).then_inc(part2_ready[name], 1)

            def split_max(unit, u):
                for g in range(2):
                    pool.wait_ge(row_max[g], STEPS * (unit + 1))
                if not (isinstance(unit, int) and unit == 0):
                    pool.wait_ge(ready["max"], unit)
                src = neg_max[u % 2]
                gp.tensor_tensor(max_parts[:, :, 0, :], src[:, :, :], zeros[:, :, :],
                                 ALU.add).then_inc(max_split, 1)
                pool.wait_ge(max_split, 3 * unit + 1)
                gp.tensor_tensor(max_rest[:, :, :], src[:, :, :], max_parts[:, :, 0, :],
                                 ALU.subtract).then_inc(max_split, 1)
                pool.wait_ge(max_split, 3 * unit + 2)
                gp.tensor_tensor(max_parts[:, :, 1, :], max_rest[:, :, :], zeros[:, :, :],
                                 ALU.add).then_inc(max_split, 1)
                pool.wait_ge(max_split, 3 * unit + 3)
                gp.tensor_tensor(max_parts[:, :, 2, :], max_rest[:, :, :], max_parts[:, :, 1, :],
                                 ALU.subtract).then_inc(max_parts_ready, 1)

            def mix(name, n):
                mu, omu = (MU_R, OMU_R) if name == "r" else (MU_K, OMU_K)
                gp.tensor_scalar(mix_a[name][:, :], xT[:, 1:1 + S], cols[:, mu:mu + 1], None, ALU.mult)
                gp.tensor_scalar(mix_b[name][:, :], xT[:, 0:S], cols[:, omu:omu + 1], None,
                                 ALU.mult).then_inc(mix_half, 1)
                pool.wait_ge(mix_half, 2 * n + (1 if name == "r" else 2))
                if not (isinstance(n, int) and n == 0):
                    pool.wait_ge(ready[f"ffn_{name}"], n)
                gp.tensor_tensor(mixed[name][:, :], mix_a[name][:, :], mix_b[name][:, :],
                                 ALU.add).then_inc(mixed_ready[name], 1)

            def square(n):
                pool.wait_ge(taken["ffn_k"], n + 1)
                if not (isinstance(n, int) and n == 0):
                    pool.wait_ge(ready["ffn_v"], n)
                gp.tensor_tensor(relu_sq[:, :], relu[:, :], relu[:, :], ALU.mult).then_inc(relu_sq_ready, 1)

            def residual(n, par):
                for t in range(T):
                    last_op = gp.tensor_tensor(x_bias[:, t, :], x_in[par][:, t, :], rows[:, 1, :], ALU.add)
                last_op.then_inc(x_bias_ready, 1)

            def add_gated(n, par):
                pool.wait_ge(taken["ffn_v"], n + 1)
                pool.wait_ge(x_bias_ready, n + 1)
                if not (isinstance(n, int) and n < 2):
                    pool.wait_ge(taken["out"], n - 1)
                gp.tensor_tensor(base[par][:, :, :], x_bias[:, :, :], gated[:, :, :],
                                 ALU.add).then_inc(base_ready, 1)

            def body(b, par):
                n, more = b + 1, not last(b)
                for s in range(SPB):
                    u = s // STEPS
                    if more and s == 3:
                        inverse_std(n)
                    if s % STEPS == 4 and (more or u < UNITS - 1):
                        split_max(UNITS * b + u + 1, u + 1)
                    if more:
                        if s == 7:
                            add_halves("k", n)
                        if s == 10:
                            rest_after_part0("k", n)
                        if s == 11:
                            part2("k", n)
                            add_halves("q", n)
                        if s == 13:
                            rest_after_part0("q", n)
                        if s == 14:
                            part2("q", n)
                            mix("r", n)
                            mix("k", n)
                        if s == 17:
                            square(n)
                            residual(n, 1 - par)
                        if s == 19:
                            add_gated(n, 1 - par)

            for buf in k_stack:
                gp.memset(buf[:, :, :], 1.0)
            gp.memset(max_cols[:, :], 0.0)
            gp.memset(zeros[:, :, :], 0.0).then_inc(fills, 1)
            pool.wait_ge(fills, 3)
            inverse_std(0)
            add_halves("k", 0)
            rest_after_part0("k", 0)
            part2("k", 0)
            add_halves("q", 0)
            rest_after_part0("q", 0)
            part2("q", 0)
            pool.wait_ge(omu_ready, 1)
            mix("r", 0)
            mix("k", 0)
            square(0)
            residual(0, 0)
            add_gated(0, 0)
            split_max(0, 0)
            batches(pool, body)




def kernel(**inputs):
    import numpy as np
    import ml_dtypes
    import concourse.bacc as bacc
    from concourse.bass_utils import run_bass_kernel_spmd

    g = {k[3:]: np.asarray(v) for k, v in inputs.items()}
    swap = np.arange(D).reshape(-1, 2)[:, ::-1].ravel()

    def w(name):
        return g[name]

    w_sq = np.stack([
        np.concatenate([w("attn_Wd_q_w"), w("attn_Wd_kv_w")], axis=1),
        w("attn_Wk_r_w"), w("attn_Wk_r_w")[:, swap], w("attn_Wo_w"),
        w("ffn_W_r").T, w("ffn_W_k").T, w("ffn_W_v").T, np.eye(D, dtype=np.float32),
    ], axis=1)
    w_lat = np.stack([
        np.concatenate([w("attn_Wu_q_w"), w("attn_Wu_k_w")], axis=0),
        np.concatenate([w("attn_Wq_r_w"), w("attn_Wu_v_w")], axis=0),
        np.concatenate([w("attn_Wq_r_w")[:, swap], np.zeros((DL, D), np.float32)], axis=0),
    ], axis=1)
    cols = np.stack([
        np.concatenate([w("attn_Wd_q_b"), w("attn_Wd_kv_b")]),
        w("attn_Wu_q_b"), w("attn_Wq_r_b"), w("attn_Wq_r_b")[swap],
        w("attn_Wu_k_b"), w("attn_Wk_r_b"), w("attn_Wk_r_b")[swap],
        w("ffn_mu_r"), w("ffn_mu_k"),
    ], axis=1)
    rows = np.stack([np.broadcast_to(w("attn_Wu_v_b"), (P, D)), np.broadcast_to(w("attn_Wo_b"), (P, D))], axis=1)
    theta = (np.float32(10000.0) ** (np.float32(-2.0) * np.arange(D // 2, dtype=np.float32))
             / np.float32(D // 2)).astype(np.float32)
    angle = (np.arange(S, dtype=np.float32)[None, :] * np.repeat(theta, 2)[:, None]).astype(np.float32)
    sign = np.where(np.arange(D) % 2 == 0, -1.0, 1.0).astype(np.float32)[:, None]
    trig = np.stack([np.cos(angle), np.sin(angle) * sign], axis=1).astype(np.float32)

    arrays = {
        "x_dram": g["attn_x"], "w_sq_dram": w_sq, "w_lat_dram": w_lat, "cols_dram": cols,
        "rows_dram": rows, "trig_dram": trig, "ident_dram": np.eye(P).astype(ml_dtypes.bfloat16),
    }
    arrays = {k: np.ascontiguousarray(v) for k, v in arrays.items()}
    nc = bacc.Bacc("TRN2", target_bir_lowering=False, num_devices=1)
    args = [nc.dram_tensor(k, v.shape, mybir.dt.from_np(v.dtype), kind="ExternalInput").ap()
            for k, v in arrays.items()]
    out = nc.dram_tensor("out_dram", (B, S, D), F32, kind="ExternalOutput").ap()
    build(nc, *args, out)
    r = run_bass_kernel_spmd(nc, [arrays], core_ids=[0])
    return r.results[0]["out_dram"]
```

```python
from contextlib import ExitStack

import concourse.bass as bass
import numpy as np
from concourse import mybir

F32 = mybir.dt.float32
BF16 = mybir.dt.bfloat16
ACT = mybir.ActivationFunctionType
ALU = mybir.AluOpType
AX_X = mybir.AxisListType.X

P = 128
B, S, D = 8, 512, 128
H = 16
HD = D // H
DL = 64
T = S // P
UNITS = 4
HPU = H // UNITS
STEPS = 8
SPB = UNITS * STEPS
LEAD = 13
RUNS = ((0, 3), (1, 2), (2, 1))
PRODUCTS = sum(n for _, n in RUNS)
USED = PRODUCTS * HD
ROWS = 96
MAX_AT = ROWS
VW = 32
EPS = 1e-5
SCALE = 1.0 / float(H + DL + DL) ** 0.5
TWO_ONES = float(np.array([0x3F803F80], np.uint32).view(np.float32)[0])
DMA = 16

DOWN, KROPE, KROPE_ROT, OUT, FFN_R, FFN_K, FFN_V, IDENT = range(8)
UP, QROPE, QROPE_ROT = range(3)
UP_V = 1
B_DOWN, B_UQ, B_QR, B_QR_ROT, B_UK, B_KR, B_KR_ROT, MU_R, MU_K, OMU_R, OMU_K = range(11)


STACKS = len(RUNS)
DCH = S * H // P
COLS_MAX = 3 * HPU * T


def build(nc, x, w_sq_dram, w_lat_dram, cols_dram, rows_dram, trig_dram, ident_dram, out):
    x_view = x.rearrange("b (t p) c -> b p t c", p=P)
    out_view = out.rearrange("b (t p) c -> b p t c", p=P)

    with ExitStack() as ctx:
        def sb(name, shape, dt=F32):
            return ctx.enter_context(nc.sbuf_tensor(name, shape, dt))

        def psum(name, shape, dt=F32):
            return ctx.enter_context(nc.psum_tensor(name, shape, dt))

        def sem(name):
            return ctx.enter_context(nc.semaphore(name))

        w_sq = sb("w_sq", [P, 8, P])
        w_lat = sb("w_lat", [P, 3, P])
        cols = sb("cols", [P, 11])
        rows = sb("rows", [P, 2, P])
        trig = sb("trig", [P, 2, S])
        ident_bf = sb("ident_bf", [P, P], BF16)
        half = sb("half", [P, T])
        x_in = [sb(f"x_in{i}", [P, T, D]) for i in range(2)]
        stats = sb("stats", [P, T, 6])
        mean_var = sb("mean_var", [P, T, 2])
        var_eps = sb("var_eps", [P, T])
        rstd = sb("rstd", [P, T])
        xn = sb("xn", [P, T, D])
        xT = sb("xT", [P, 1 + S])
        latT = sb("latT", [P, S])
        rot_c = {n: sb(f"{n}_rot_c", [P, S]) for n in "qk"}
        rot_s = {n: sb(f"{n}_rot_s", [P, S]) for n in "qk"}
        rot = {n: sb(f"{n}_rot", [P, S]) for n in "qk"}
        full = {n: sb(f"{n}_full", [P, S]) for n in "qk"}
        rest = {n: sb(f"{n}_rest", [P, S]) for n in "qk"}
        parts = {n: sb(f"{n}_parts", [P, 3, S], BF16) for n in "qk"}
        q_stack = [sb(f"q_stack{i}", [P, H, S], BF16) for i in range(2)]
        k_stack = [sb(f"k_stack{i}", [P, H, S], BF16) for i in range(2)]
        vals = [sb(f"vals{i}", [P, T, H, VW]) for i in range(2)]
        probs = sb("probs", [P, STEPS, 2, S])
        neg_max = [sb(f"neg_max{i}", [P, HPU * T]) for i in range(2)]
        max_rest = sb("max_rest", [P, HPU * T])
        max_cols = sb("max_cols", [P, P], BF16)
        max_parts = max_cols[:, 0:COLS_MAX].rearrange("p (k c) -> p k c", k=3)
        zeros = sb("zeros", [P, HPU * T])
        max_rows = [sb(f"max_rows{i}", [COLS_MAX, P], BF16) for i in range(2)]
        pv = [sb(f"pv{i}", [P, S]) for i in range(2)]
        num = sb("num", [P, S])
        den = sb("den", [P, DCH])
        rden_c = sb("rden_c", [P, DCH])
        rden = sb("rden", [P, S])
        attnT = sb("attnT", [P, S])
        mix_a = {n: sb(f"mix_a_{n}", [P, S]) for n in "rk"}
        mix_b = {n: sb(f"mix_b_{n}", [P, S]) for n in "rk"}
        mixed = {n: sb(f"mixed_{n}", [P, S]) for n in "rk"}
        gate = sb("gate", [P, T, D])
        relu = sb("relu", [P, S])
        relu_sq = sb("relu_sq", [P, S])
        gated = sb("gated", [P, T, D])
        x_bias = sb("x_bias", [P, T, D])
        base = [sb(f"base{i}", [P, T, D]) for i in range(2)]
        y = sb("y", [P, T, D])

        ps_max = [psum(f"ps_max{i}", [P, 2, S]) for i in range(2)]
        ps_exp = [psum(f"ps_exp{g}", [P, S]) for g in range(2)]
        ps_pv = psum("ps_pv", [P, S])
        ps_misc = psum("ps_misc", [P, S])
        ps_misc_bf = ps_misc[:, :].bitcast(BF16)
        ps_tok = ps_misc[:, :].rearrange("p (t c) -> p t c", t=T)

        spills = {n: nc.dram_tensor(f"{n}_spill", (3, HD, H, S), BF16, kind="Internal").ap() for n in "qk"}
        pv_spill = nc.dram_tensor("pv_spill", (UNITS, HPU, VW, S), F32, kind="Internal").ap()
        rden_spill = nc.dram_tensor("rden_spill", (H, S), F32, kind="Internal").ap()

        consts_in = sem("consts_in")
        fills = sem("fills")
        cleared = sem("cleared")
        omu_ready = sem("omu_ready")
        x_landed = sem("x_landed")
        stats_ready = sem("stats_ready")
        mv_ready = sem("mv_ready")
        var_ready = sem("var_ready")
        rstd_ready = sem("rstd_ready")
        xn_ready = sem("xn_ready")
        JOBS = ("xT", "k_cos", "k_sin", "lat", "k_lin", "q_cos", "q_sin", "q_lin", "vals",
                "ffn_r", "ffn_k", "ffn_v", "out", "max")
        ready = {n: sem(f"{n}_ready") for n in JOBS}
        taken = {n: sem(f"{n}_taken") for n in JOBS}
        rot_ready = {n: sem(f"{n}_rot_ready") for n in "qk"}
        part0_ready = {n: sem(f"{n}_part0_ready") for n in "qk"}
        rest_ready = {n: sem(f"{n}_rest_ready") for n in "qk"}
        part1_ready = {n: sem(f"{n}_part1_ready") for n in "qk"}
        part2_ready = {n: sem(f"{n}_part2_ready") for n in "qk"}
        spilled = {n: sem(f"{n}_spilled") for n in "qk"}
        stacked = {n: sem(f"{n}_stacked") for n in "qk"}
        mix_half = sem("mix_half")
        mixed_ready = {n: sem(f"mixed_{n}_ready") for n in "rk"}
        relu_sq_ready = sem("relu_sq_ready")
        x_bias_ready = sem("x_bias_ready")
        base_ready = sem("base_ready")
        raw_scores = sem("raw_scores")
        row_max = sem("row_max")
        max_split = sem("max_split")
        max_parts_ready = sem("max_parts_ready")
        max_stacked = [sem(f"max_stacked{i}") for i in range(2)]
        scores_ready = [sem(f"scores_ready{g}") for g in range(2)]
        probs_ready = [sem(f"probs_ready{g}") for g in range(2)]
        pv_done = sem("pv_done")
        pv_taken = sem("pv_taken")
        pv_spilled = [sem(f"pv_spilled{i}") for i in range(2)]
        pv_gathered = sem("pv_gathered")
        rden_ready = sem("rden_ready")
        rden_spilled = sem("rden_spilled")
        rden_spread = sem("rden_spread")
        attn_ready = sem("attn_ready")
        stored = sem("stored")

        block = ctx.enter_context(nc.Block())


        def batches(eng, body):
            body(0, 0)
            with eng.Fori(0, (B - 2) // 2) as i:
                body(2 * i + 1, 1)
                body(2 * i + 2, 0)
            body(B - 1, 1)
            body(B, 0)

        def steps(b, par):
            for o in range(STEPS if ended(b) else SPB):
                if o >= STEPS:
                    yield o, b, par, o - STEPS
                else:
                    yield o, b - 1, 1 - par, o + SPB - STEPS

        def softmax_begun(c):
            return not (isinstance(c, int) and c < 0)

        def ended(b):
            return isinstance(b, int) and b == B

        def first(b):
            return isinstance(b, int) and b == 0

        def last(b):
            return isinstance(b, int) and b >= B - 1

        @block.sync
        def _(sp):
            def value(count):
                if not isinstance(count, int):
                    sp.compute_val(count)
                return count

            def load_x(n, par):
                sp.dma_start(x_in[par][:, :, :], x_view[n]).then_inc(x_landed, DMA)

            def spill(name, n):
                copies_read = value(STACKS * DMA * n)
                sp.wait_ge(part2_ready[name], n + 1)
                if not (isinstance(n, int) and n == 0):
                    sp.wait_ge(stacked[name], copies_read)
                for part in range(3):
                    sp.dma_start(spills[name][part].rearrange("d h q -> h d q"),
                                 parts[name][:, part, :]).then_inc(spilled[name], DMA)

            def stack(name, n, par):
                scores_read = value(SPB * (n - 1))
                sp.wait_ge(spilled[name], 3 * DMA * (n + 1))
                if not (isinstance(n, int) and n < 2):
                    sp.wait_ge(scores_ready[1], scores_read)
                dst = (q_stack if name == "q" else k_stack)[par]
                at = 0
                for q_part, count in RUNS:
                    if name == "q":
                        src = spills[name][q_part:q_part + 1].to_broadcast([count, HD, H, S])
                    else:
                        src = spills[name][0:count]
                    sp.dma_start(dst[at:at + HD * count, :, :], src).then_inc(stacked[name], DMA)
                    at += HD * count

            def stack_max(unit, u, par, x_read=None):
                sp.wait_ge(taken["max"], unit + 1)
                if x_read is not None:
                    sp.wait_ge(x_bias_ready, x_read)
                sp.dma_start(q_stack[par][MAX_AT:MAX_AT + 3, HPU * u:HPU * (u + 1), :],
                             max_rows[u % 2][:, :]).then_inc(max_stacked[u % 2], DMA)

            def spill_pv(b, u):
                sp.wait_ge(pv_taken, UNITS * b + u + 1)
                if u == 0 and not first(b):
                    sp.wait_ge(pv_gathered, 2 * DMA * b)
                sp.dma_start(pv_spill[u].rearrange("j r q -> (j r) q"),
                             pv[u % 2][:, :]).then_inc(pv_spilled[u % 2], DMA)

            def gather(b):
                attn_read = value(b)
                for spilled_half in pv_spilled:
                    sp.wait_ge(spilled_half, UNITS // 2 * DMA * (b + 1))
                if not first(b):
                    sp.wait_ge(attn_ready, attn_read)
                strips = pv_spill.rearrange("u j r q -> (u j) r q")
                sp.dma_start(num[:, :], strips[:, 0:HD, :]).then_inc(pv_gathered, DMA)
                sp.dma_start(den[:, :], strips[:, HD:HD + 1, :].rearrange("h o (k q) -> h (o k) q", q=DCH)
                             ).then_inc(pv_gathered, DMA)

            def spread_inverse(b):
                sp.wait_ge(rden_ready, b + 1)
                sp.dma_start(rden_spill.rearrange("h (k q) -> (h k) q", q=DCH),
                             rden_c[:, :]).then_inc(rden_spilled, DMA)
                sp.wait_ge(rden_spilled, DMA * (b + 1))
                src = rden_spill.rearrange("(h o) q -> h o q", o=1).to_broadcast([H, HD, S])
                sp.dma_start(rden[:, :], src).then_inc(rden_spread, DMA)

            def store(b):
                sp.wait_ge(taken["out"], b + 1)
                sp.dma_start(out_view[b], y[:, :, :]).then_inc(stored, DMA)

            def body(b, par):
                for o, c, cpar, s in steps(b, par):
                    more = not last(b)
                    if o == 0 and more:
                        load_x(b + 1, 1 - par)
                    if o % STEPS == 3 and softmax_begun(c) and s >= STEPS:
                        spill_pv(c, s // STEPS - 1)
                    elif o == 11 and not first(b):
                        spill_pv(b - 1, UNITS - 1)
                        gather(b - 1)
                    if o % STEPS == 5 and not ended(b):
                        stack_max(UNITS * b + o // STEPS, o // STEPS, par,
                                  x_read=b + 1 if o == 29 else None)
                    if more:
                        if o == 15:
                            spill("k", b + 1)
                        if o == 16:
                            stack("k", b + 1, 1 - par)
                        if o == 21:
                            spill("q", b + 1)
                        if o == 22:
                            stack("q", b + 1, 1 - par)
                    if not first(b) and not ended(b):
                        if o == 15:
                            spread_inverse(b - 1)
                        if o == 24:
                            store(b - 1)

            sp.dma_start(x_in[0][:, :, :], x_view[0]).then_inc(x_landed, DMA)
            sp.dma_start(w_sq[:, :, :], w_sq_dram).then_inc(consts_in, DMA)
            sp.dma_start(cols[:, 0:9], cols_dram).then_inc(consts_in, DMA)
            sp.dma_start(trig[:, :, :], trig_dram).then_inc(consts_in, DMA)
            sp.dma_start(w_lat[:, :, :], w_lat_dram).then_inc(consts_in, DMA)
            sp.dma_start(rows[:, :, :], rows_dram).then_inc(consts_in, DMA)
            sp.dma_start(ident_bf[:, :], ident_dram).then_inc(consts_in, DMA)
            sp.wait_ge(fills, 3)
            for name in "kq":
                spill(name, 0)
                stack(name, 0, 0)
            batches(sp, body)
            spill_pv(B - 1, UNITS - 1)
            gather(B - 1)
            spread_inverse(B - 1)
            store(B - 1)
            sp.wait_ge(stored, DMA * B)

        CONSTS = 6 * DMA

        @block.tensor
        def _(pe):
            mm = nc.tensor.matmul

            def project(job, w, rhs):
                mm(ps_misc[:, :], w, rhs, start=True, stop=True).then_inc(ready[job], 1)

            def transpose_x(n):
                pe.wait_ge(xn_ready, n + 1)
                if not (isinstance(n, int) and n == 0):
                    pe.wait_ge(taken["max"], UNITS * (n - 1) + 1)
                for t in range(T):
                    last_mm = nc.tensor.transpose(ps_tok[:, t, :], xn[:, t, :], w_sq[:, IDENT, :])
                last_mm.then_inc(ready["xT"], 1)

            def k_cos(n):
                pe.wait_ge(taken["xT"], n + 1)
                project("k_cos", w_sq[:, KROPE, :], xT[:, 1:1 + S])

            def k_sin(n):
                pe.wait_ge(taken["k_cos"], n + 1)
                project("k_sin", w_sq[:, KROPE_ROT, :], xT[:, 1:1 + S])

            def latents(n):
                pe.wait_ge(taken["k_sin"], n + 1)
                project("lat", w_sq[:, DOWN, :], xT[:, 1:1 + S])

            def k_lin(n):
                pe.wait_ge(taken["lat"], n + 1)
                project("k_lin", w_lat[DL:P, UP, :], latT[DL:P, :])

            def q_cos(n):
                if isinstance(n, int) and n == 0:
                    pe.wait_ge(taken["k_lin"], 1)
                else:
                    pe.wait_ge(taken["max"], UNITS * (n - 1) + 2)
                project("q_cos", w_lat[0:DL, QROPE, :], latT[0:DL, :])

            def q_sin(n):
                pe.wait_ge(taken["q_cos"], n + 1)
                project("q_sin", w_lat[0:DL, QROPE_ROT, :], latT[0:DL, :])

            def q_lin(n):
                pe.wait_ge(taken["q_sin"], n + 1)
                project("q_lin", w_lat[0:DL, UP, :], latT[0:DL, :])

            def values(n):
                pe.wait_ge(taken["q_lin"], n + 1)
                for t in range(T):
                    last_mm = mm(ps_tok[:, t, :], latT[DL:P, t * P:(t + 1) * P], w_lat[DL:P, UP_V, :],
                                 start=True, stop=True)
                last_mm.then_inc(ready["vals"], 1)

            def ffn_r(n, before):
                pe.wait_ge(*before)
                pe.wait_ge(mixed_ready["r"], n + 1)
                for t in range(T):
                    last_mm = mm(ps_tok[:, t, :], mixed["r"][:, t * P:(t + 1) * P], w_sq[:, FFN_R, :],
                                 start=True, stop=True)
                last_mm.then_inc(ready["ffn_r"], 1)

            def ffn_k(n):
                pe.wait_ge(taken["ffn_r"], n + 1)
                pe.wait_ge(mixed_ready["k"], n + 1)
                project("ffn_k", w_sq[:, FFN_K, :], mixed["k"][:, :])

            def ffn_v(n, before):
                pe.wait_ge(*before)
                pe.wait_ge(relu_sq_ready, n + 1)
                for t in range(T):
                    last_mm = mm(ps_tok[:, t, :], relu_sq[:, t * P:(t + 1) * P], w_sq[:, FFN_V, :],
                                 start=True, stop=True)
                last_mm.then_inc(ready["ffn_v"], 1)

            def transpose_max(unit, before):
                pe.wait_ge(*before)
                pe.wait_ge(max_parts_ready, unit + 1)
                nc.tensor.transpose(ps_misc_bf[:, 0:P], max_cols[:, :], ident_bf[:, :]).then_inc(ready["max"], 1)

            def out_projection(b, before):
                pe.wait_ge(*before)
                pe.wait_ge(attn_ready, b + 1)
                for t in range(T):
                    last_mm = mm(ps_tok[:, t, :], attnT[:, t * P:(t + 1) * P], w_sq[:, OUT, :],
                                 start=True, stop=True)
                last_mm.then_inc(ready["out"], 1)

            def scores_for_max(b, par, r):
                if r == 0:
                    pe.wait_ge(stacked["k"], STACKS * DMA * (b + 1))
                    pe.wait_ge(stacked["q"], STACKS * DMA * (b + 1))
                if not (first(b) and r < 2):
                    pe.wait_ge(row_max, SPB * b + r - 1)
                for g in range(2):
                    head, qt = 2 * (r // T) + g, r % T
                    last_mm = mm(ps_max[r % 2][:, g, :], q_stack[par][0:ROWS, head, qt * P:(qt + 1) * P],
                                 k_stack[par][0:ROWS, head, :], start=True, stop=True)
                last_mm.then_inc(raw_scores, 1)

            def scores_for_exp(b, par, s, g):
                u, kt, pp = s // STEPS, s % STEPS // 2, s % 2
                if s % STEPS == 0 and g == 0:
                    pe.wait_ge(max_stacked[u % 2], DMA * (UNITS // 2 * b + u // 2 + 1))
                if not (first(b) and s < 1):
                    pe.wait_ge(probs_ready[g], SPB * b + s)
                head = HPU * u + 2 * pp + g
                mm(ps_exp[g][:, :], k_stack[par][:, head, kt * P:(kt + 1) * P],
                   q_stack[par][:, head, :], start=True, stop=True).then_inc(scores_ready[g], 1)

            def probs_values(b, par, u, kt):
                pe.wait_ge(probs_ready[1], SPB * b + STEPS * u + 2 * kt + 2)
                if kt == 0 and not (first(b) and u == 0):
                    pe.wait_ge(pv_taken, UNITS * b + u)
                for j in range(HPU):
                    last_mm = mm(ps_pv[VW * j:VW * (j + 1), :], vals[par][:, kt, HPU * u + j, :],
                                 probs[:, 2 * kt + j // 2, j % 2, :], start=kt == 0, stop=kt == T - 1)
                last_mm.then_inc(pv_done, 1)

            def ahead(b, par, s):
                r = s + LEAD
                if r < SPB:
                    scores_for_max(b, par, r)
                elif not last(b):
                    scores_for_max(b + 1, 1 - par, r - SPB)

            def body(b, par):
                n, more = b + 1, not last(b)
                for o, c, cpar, s in steps(b, par):
                    if softmax_begun(c):
                        scores_for_exp(c, cpar, s, 0)
                    ahead(c, cpar, s)
                    if softmax_begun(c):
                        u = s // STEPS
                        if s % STEPS in (3, 5, 7):
                            probs_values(c, cpar, u, (s % STEPS - 3) // 2)
                        elif s % STEPS == 1 and s > 1:
                            probs_values(c, cpar, u - 1, T - 1)
                        elif s == 1 and not first(c):
                            probs_values(c - 1, 1 - cpar, UNITS - 1, T - 1)
                        scores_for_exp(c, cpar, s, 1)
                    if ended(b):
                        continue
                    if o == 5:
                        transpose_max(UNITS * b, (taken["ffn_v"], b + 1))
                    if o == 13:
                        transpose_max(UNITS * b + 1, (taken["k_lin"], n + 1) if more
                                      else (taken["max"], UNITS * b + 1))
                    if o == 21:
                        transpose_max(UNITS * b + 2, (taken["vals"], n + 1) if more
                                      else (taken["max"], UNITS * b + 2))
                    if o == 22 and not first(b):
                        out_projection(b - 1, (taken["max"], UNITS * b + 3))
                    if o == 29:
                        transpose_max(UNITS * b + 3, (taken["ffn_k"], n + 1) if more
                                      else (taken["out"], b))
                    if more:
                        if o == 5:
                            transpose_x(n)
                        if o == 7:
                            k_cos(n)
                        if o == 9:
                            k_sin(n)
                        if o == 10:
                            latents(n)
                        if o == 12:
                            k_lin(n)
                        if o == 14:
                            q_cos(n)
                        if o == 16:
                            q_sin(n)
                        if o == 18:
                            q_lin(n)
                        if o == 20:
                            values(n)
                        if o == 24:
                            ffn_r(n, (taken["max"], UNITS * b + 3) if first(b) else (taken["out"], b))
                        if o == 26:
                            ffn_k(n)
                        if o == 30:
                            ffn_v(n, (taken["max"], UNITS * b + 4))

            pe.wait_ge(consts_in, CONSTS)
            pe.wait_ge(fills, 3)
            transpose_x(0)
            k_cos(0)
            k_sin(0)
            latents(0)
            k_lin(0)
            q_cos(0)
            q_sin(0)
            q_lin(0)
            values(0)
            ffn_r(0, (taken["vals"], 1))
            ffn_k(0)
            for r in range(LEAD - STEPS):
                scores_for_max(0, 0, r)
            ffn_v(0, (taken["ffn_k"], 1))
            batches(pe, body)
            probs_values(B - 1, 1, UNITS - 1, T - 1)
            out_projection(B - 1, (taken["max"], UNITS * B))

        @block.scalar
        def _(act):
            activation = nc.scalar.activation

            def take_xT(n):
                act.wait_ge(ready["xT"], n + 1)
                if not (isinstance(n, int) and n == 0):
                    act.wait_ge(ready["lat"], n)
                    act.wait_ge(mixed_ready["k"], n)
                activation(xT[:, 1:1 + S], ps_misc[:, :], ACT.Copy).then_inc(taken["xT"], 1)

            def take_latents(n):
                act.wait_ge(ready["lat"], n + 1)
                if not (isinstance(n, int) and n == 0):
                    act.wait_ge(ready["vals"], n)
                activation(latT[:, :], ps_misc[:, :], ACT.Identity,
                           bias=cols[:, B_DOWN:B_DOWN + 1]).then_inc(taken["lat"], 1)

            def part0(name, n):
                act.wait_ge(taken[f"{name}_lin"], n + 1)
                if not (isinstance(n, int) and n == 0):
                    act.wait_ge(stacked[name], STACKS * DMA * n)
                activation(parts[name][:, 0, :], full[name][:, :], ACT.Copy).then_inc(part0_ready[name], 1)

            def part1(name, n):
                act.wait_ge(rest_ready[name], n + 1)
                activation(parts[name][:, 1, :], rest[name][:, :], ACT.Copy).then_inc(part1_ready[name], 1)

            def take_max(b, u):
                act.wait_ge(ready["max"], UNITS * b + u + 1)
                if not (first(b) and u < 2):
                    act.wait_ge(max_stacked[u % 2], DMA * (UNITS // 2 * b + u // 2))
                activation(max_rows[u % 2][:, :], ps_misc_bf[0:COLS_MAX, 0:P], ACT.Copy).then_inc(taken["max"], 1)

            def take_ffn_r(n):
                act.wait_ge(ready["ffn_r"], n + 1)
                if not (isinstance(n, int) and n == 0):
                    act.wait_ge(taken["ffn_v"], n)
                activation(gate[:, :, :], ps_tok, ACT.Tanh, scale=0.5).then_inc(taken["ffn_r"], 1)

            def take_ffn_k(n):
                act.wait_ge(ready["ffn_k"], n + 1)
                if not (isinstance(n, int) and n == 0):
                    act.wait_ge(relu_sq_ready, n)
                activation(relu[:, :], ps_misc[:, :], ACT.Relu).then_inc(taken["ffn_k"], 1)

            def softmax_exp(b, s):
                for g in range(2):
                    act.wait_ge(scores_ready[g], SPB * b + s + 1)
                    if g == 0 and not (first(b) and s < STEPS):
                        act.wait_ge(pv_done, T * (UNITS * b + s // STEPS - 1) + s % STEPS // 2 + 1)
                    activation(probs[:, s % STEPS, g, :], ps_exp[g][:, :], ACT.Exp,
                               scale=SCALE).then_inc(probs_ready[g], 1)

            def take_pv(b, u):
                act.wait_ge(pv_done, T * (UNITS * b + u + 1))
                if not (first(b) and u < 2):
                    act.wait_ge(pv_spilled[u % 2], DMA * (UNITS // 2 * b + u // 2))
                activation(pv[u % 2][:, :], ps_pv[:, :], ACT.Copy).then_inc(pv_taken, 1)

            def body(b, par):
                n, more = b + 1, not last(b)
                for o, c, cpar, s in steps(b, par):
                    if softmax_begun(c):
                        softmax_exp(c, s)
                        if s % STEPS == 2 and s > 2:
                            take_pv(c, s // STEPS - 1)
                        elif s == 2 and not first(c):
                            take_pv(c - 1, UNITS - 1)
                    if o % STEPS == 5 and not ended(b):
                        take_max(b, o // STEPS)
                    if more:
                        if o == 5:
                            take_xT(n)
                        if o == 10:
                            take_latents(n)
                        if o == 13:
                            part0("k", n)
                        if o == 14:
                            part1("k", n)
                        if o == 19:
                            part0("q", n)
                        if o == 20:
                            part1("q", n)
                        if o == 24:
                            take_ffn_r(n)
                        if o == 26:
                            take_ffn_k(n)

            act.wait_ge(consts_in, CONSTS)
            take_xT(0)
            take_latents(0)
            part0("k", 0)
            part1("k", 0)
            part0("q", 0)
            part1("q", 0)
            take_ffn_r(0)
            take_ffn_k(0)
            batches(act, body)
            take_pv(B - 1, UNITS - 1)

        @block.vector
        def _(dve):
            vec = nc.vector

            def layer_norm_stats(n, par):
                dve.wait_ge(x_landed, DMA * (n + 1))
                for t in range(T):
                    last_op = vec.bn_stats(stats[:, t, :], x_in[par][:, t, :])
                last_op.then_inc(stats_ready, 1)

            def mean_variance(n):
                for t in range(T):
                    last_op = vec.bn_aggr(mean_var[:, t, :], stats[:, t, :])
                last_op.then_inc(mv_ready, 1)
                dve.wait_ge(mv_ready, n + 1)
                vec.tensor_scalar(var_eps[:, :], mean_var[:, :, 1], EPS, None, ALU.add).then_inc(var_ready, 1)

            def layer_norm(n, par):
                dve.wait_ge(rstd_ready, n + 1)
                if not (isinstance(n, int) and n == 0):
                    dve.wait_ge(ready["xT"], n)
                for t in range(T):
                    last_op = vec.tensor_scalar(xn[:, t, :], x_in[par][:, t, :], mean_var[:, t, 0:1],
                                                rstd[:, t:t + 1], ALU.subtract, ALU.mult)
                last_op.then_inc(xn_ready, 1)

            def rope_half(name, which, n):
                job = f"{name}_{which}"
                dve.wait_ge(ready[job], n + 1)
                if not (isinstance(n, int) and n == 0):
                    dve.wait_ge(rot_ready[name], n)
                bias = {"q_cos": B_QR, "q_sin": B_QR_ROT, "k_cos": B_KR, "k_sin": B_KR_ROT}[job]
                dst = (rot_c if which == "cos" else rot_s)[name]
                vec.scalar_tensor_tensor(dst[:, :], ps_misc[:, :], cols[:, bias:bias + 1],
                                         trig[:, 0 if which == "cos" else 1, :],
                                         ALU.add, ALU.mult).then_inc(taken[job], 1)

            def add_linear(name, n):
                dve.wait_ge(ready[f"{name}_lin"], n + 1)
                dve.wait_ge(rot_ready[name], n + 1)
                if not (isinstance(n, int) and n == 0):
                    dve.wait_ge(rest_ready[name], n)
                bias = B_UQ if name == "q" else B_UK
                vec.scalar_tensor_tensor(full[name][:, :], ps_misc[:, :], cols[:, bias:bias + 1],
                                         rot[name][:, :], ALU.add, ALU.add).then_inc(taken[f"{name}_lin"], 1)

            def take_values(n, par):
                dve.wait_ge(ready["vals"], n + 1)
                if not (isinstance(n, int) and n < 2):
                    dve.wait_ge(pv_done, T * UNITS * (n - 1))
                for t in range(T):
                    last_op = vec.tensor_tensor(vals[par][:, t, :, 0:HD],
                                                ps_tok[:, t, :].rearrange("p (h d) -> p h d", d=HD),
                                                rows[:, 0, :].rearrange("p (h d) -> p h d", d=HD), ALU.add)
                last_op.then_inc(taken["vals"], 1)

            def take_ffn_v(n):
                dve.wait_ge(ready["ffn_v"], n + 1)
                dve.wait_ge(taken["ffn_r"], n + 1)
                if not (isinstance(n, int) and n == 0):
                    dve.wait_ge(base_ready, n)
                vec.scalar_tensor_tensor(gated[:, :, :], gate[:, :, :], 1.0, ps_tok,
                                         ALU.add, ALU.mult).then_inc(taken["ffn_v"], 1)

            def invert(b):
                dve.wait_ge(pv_gathered, 2 * DMA * (b + 1))
                if not first(b):
                    dve.wait_ge(rden_spilled, DMA * b)
                vec.reciprocal(rden_c[:, :], den[:, :]).then_inc(rden_ready, 1)

            def normalise(b):
                dve.wait_ge(rden_spread, DMA * (b + 1))
                if not first(b):
                    dve.wait_ge(ready["out"], b)
                vec.tensor_tensor(attnT[:, :], num[:, :], rden[:, :], ALU.mult).then_inc(attn_ready, 1)

            def finish(b, par):
                dve.wait_ge(ready["out"], b + 1)
                dve.wait_ge(base_ready, b + 1)
                if not first(b):
                    dve.wait_ge(stored, DMA * b)
                vec.tensor_tensor(y[:, :, :], ps_tok, base[par][:, :, :], ALU.add).then_inc(taken["out"], 1)

            def reduce_rows(b, r):
                unit, c = r // STEPS, r % STEPS
                dve.wait_ge(raw_scores, SPB * b + r + 1)
                if c == 0 and not (first(b) and unit < 2):
                    dve.wait_ge(max_parts_ready, UNITS * b + unit - 1)
                pair, qt = c // T, c % T
                dst = neg_max[unit % 2][:, :].rearrange("p (h t) -> p h t", t=T)
                vec.tensor_reduce(dst[:, 2 * pair:2 * pair + 2, qt], ps_max[r % 2][:, :, :], AX_X, ALU.max,
                                  negate=True).then_inc(row_max, 1)

            def ahead(b, s):
                r = s + LEAD
                if r < SPB:
                    reduce_rows(b, r)
                elif not last(b):
                    reduce_rows(b + 1, r - SPB)

            def body(b, par):
                n, more = b + 1, not last(b)
                for o, c, cpar, s in steps(b, par):
                    if more and o == 3:
                        dve.wait_ge(stats_ready, n + 1)
                    ahead(c, s)
                    if not first(b) and not ended(b):
                        if o == 14:
                            invert(b - 1)
                        if o == 21:
                            normalise(b - 1)
                        if o == 22:
                            finish(b - 1, 1 - par)
                    if more:
                        if o == 2:
                            layer_norm_stats(n, 1 - par)
                        if o == 3:
                            mean_variance(n)
                        if o == 4:
                            layer_norm(n, 1 - par)
                        if o == 7:
                            rope_half("k", "cos", n)
                        if o == 9:
                            rope_half("k", "sin", n)
                        if o == 12:
                            add_linear("k", n)
                        if o == 14:
                            rope_half("q", "cos", n)
                        if o == 16:
                            rope_half("q", "sin", n)
                        if o == 18:
                            add_linear("q", n)
                        if o == 20:
                            take_values(n, 1 - par)
                        if o == 30:
                            take_ffn_v(n)

            for buf in vals:
                vec.memset(buf[:, :, :, :], 1.0)
            vec.memset(half[:, :], -0.5)
            vec.memset(xT[:, 0:1], 0.0).then_inc(fills, 1)
            dve.wait_ge(consts_in, CONSTS)
            vec.tensor_scalar(cols[:, OMU_R:OMU_K + 1], cols[:, MU_R:MU_K + 1], -1.0, 1.0,
                              ALU.mult, ALU.add).then_inc(omu_ready, 1)
            vec.tensor_scalar(w_sq[:, FFN_V, :], w_sq[:, FFN_V, :], 0.5, None, ALU.mult).then_inc(fills, 1)
            layer_norm_stats(0, 0)
            dve.wait_ge(stats_ready, 1)
            mean_variance(0)
            layer_norm(0, 0)
            rope_half("k", "cos", 0)
            rope_half("k", "sin", 0)
            add_linear("k", 0)
            rope_half("q", "cos", 0)
            rope_half("q", "sin", 0)
            add_linear("q", 0)
            take_values(0, 0)
            for r in range(LEAD - STEPS):
                reduce_rows(0, r)
            take_ffn_v(0)
            batches(dve, body)
            invert(B - 1)
            normalise(B - 1)
            finish(B - 1, 1)

        @block.gpsimd
        def _(pool):
            gp = nc.gpsimd

            def inverse_std(n):
                pool.wait_ge(var_ready, n + 1)
                gp.tensor_tensor(rstd[:, :], var_eps[:, :], half[:, :], ALU.pow).then_inc(rstd_ready, 1)

            def add_halves(name, n):
                pool.wait_ge(taken[f"{name}_sin"], n + 1)
                if not (isinstance(n, int) and n == 0):
                    pool.wait_ge(taken[f"{name}_lin"], n)
                gp.tensor_tensor(rot[name][:, :], rot_c[name][:, :], rot_s[name][:, :],
                                 ALU.add).then_inc(rot_ready[name], 1)

            def rest_after_part0(name, n):
                pool.wait_ge(part0_ready[name], n + 1)
                gp.tensor_tensor(rest[name][:, :], full[name][:, :], parts[name][:, 0, :],
                                 ALU.subtract).then_inc(rest_ready[name], 1)

            def part2(name, n):
                pool.wait_ge(part1_ready[name], n + 1)
                gp.tensor_tensor(parts[name][:, 2, :], rest[name][:, :], parts[name][:, 1, :],
                                 ALU.subtract).then_inc(part2_ready[name], 1)

            def split_max(unit, u):
                pool.wait_ge(row_max, STEPS * (unit + 1))
                if not (isinstance(unit, int) and unit == 0):
                    pool.wait_ge(ready["max"], unit)
                src = neg_max[u % 2]
                gp.tensor_tensor(max_parts[:, 0, :], src[:, :], zeros[:, :],
                                 ALU.add).then_inc(max_split, 1)
                pool.wait_ge(max_split, 3 * unit + 1)
                gp.tensor_tensor(max_rest[:, :], src[:, :], max_parts[:, 0, :],
                                 ALU.subtract).then_inc(max_split, 1)
                pool.wait_ge(max_split, 3 * unit + 2)
                gp.tensor_tensor(max_parts[:, 1, :], max_rest[:, :], zeros[:, :],
                                 ALU.add).then_inc(max_split, 1)
                pool.wait_ge(max_split, 3 * unit + 3)
                gp.tensor_tensor(max_parts[:, 2, :], max_rest[:, :], max_parts[:, 1, :],
                                 ALU.subtract).then_inc(max_parts_ready, 1)

            def mix(name, n):
                mu, omu = (MU_R, OMU_R) if name == "r" else (MU_K, OMU_K)
                gp.tensor_scalar(mix_a[name][:, :], xT[:, 1:1 + S], cols[:, mu:mu + 1], 0.0,
                                 ALU.mult, ALU.add)
                gp.tensor_scalar(mix_b[name][:, :], xT[:, 0:S], cols[:, omu:omu + 1], 0.0,
                                 ALU.mult, ALU.add).then_inc(mix_half, 1)
                pool.wait_ge(mix_half, 2 * n + (1 if name == "r" else 2))
                if not (isinstance(n, int) and n == 0):
                    pool.wait_ge(ready[f"ffn_{name}"], n)
                gp.tensor_tensor(mixed[name][:, :], mix_a[name][:, :], mix_b[name][:, :],
                                 ALU.add).then_inc(mixed_ready[name], 1)

            def square(n):
                pool.wait_ge(taken["ffn_k"], n + 1)
                if not (isinstance(n, int) and n == 0):
                    pool.wait_ge(ready["ffn_v"], n)
                gp.tensor_tensor(relu_sq[:, :], relu[:, :], relu[:, :], ALU.mult).then_inc(relu_sq_ready, 1)

            def residual(n, par):
                for t in range(T):
                    last_op = gp.tensor_tensor(x_bias[:, t, :], x_in[par][:, t, :], rows[:, 1, :], ALU.add)
                last_op.then_inc(x_bias_ready, 1)

            def add_gated(n, par):
                pool.wait_ge(taken["ffn_v"], n + 1)
                pool.wait_ge(x_bias_ready, n + 1)
                if not (isinstance(n, int) and n < 2):
                    pool.wait_ge(taken["out"], n - 1)
                gp.tensor_tensor(base[par][:, :, :], x_bias[:, :, :], gated[:, :, :],
                                 ALU.add).then_inc(base_ready, 1)

            def body(b, par):
                n, more = b + 1, not last(b)
                for o, c, cpar, s in steps(b, par):
                    if o % STEPS == 3 and not ended(b):
                        split_max(UNITS * b + o // STEPS, o // STEPS)
                    if more:
                        if o == 3:
                            inverse_std(n)
                        if o == 9:
                            add_halves("k", n)
                        if o == 13:
                            rest_after_part0("k", n)
                        if o == 14:
                            part2("k", n)
                            mix("r", n)
                        if o == 16:
                            add_halves("q", n)
                            mix("k", n)
                        if o == 19:
                            rest_after_part0("q", n)
                        if o == 20:
                            part2("q", n)
                        if o == 26:
                            square(n)
                            residual(n, 1 - par)
                        if o == 30:
                            add_gated(n, 1 - par)

            def clear_stacks(par):
                gp.memset(q_stack[par][:, :, :].bitcast(F32), 0.0)
                gp.memset(k_stack[par][:, :, :].bitcast(F32), 0.0).then_inc(cleared, 1)
                pool.wait_ge(cleared, 2 * par + 1)
                gp.memset(k_stack[par][MAX_AT:P, :, :].bitcast(F32), TWO_ONES).then_inc(cleared, 1)
                pool.wait_ge(cleared, 2 * par + 2)

            clear_stacks(0)
            gp.memset(max_cols[:, :], 0.0)
            gp.memset(zeros[:, :], 0.0).then_inc(fills, 1)
            pool.wait_ge(fills, 3)
            inverse_std(0)
            add_halves("k", 0)
            rest_after_part0("k", 0)
            part2("k", 0)
            add_halves("q", 0)
            rest_after_part0("q", 0)
            part2("q", 0)
            pool.wait_ge(omu_ready, 1)
            mix("r", 0)
            mix("k", 0)
            square(0)
            residual(0, 0)
            add_gated(0, 0)
            clear_stacks(1)
            batches(pool, body)




def kernel(**inputs):
    import ml_dtypes
    import concourse.bacc as bacc
    from concourse.bass_utils import run_bass_kernel_spmd

    g = {k[3:]: np.asarray(v) for k, v in inputs.items()}
    swap = np.arange(D).reshape(-1, 2)[:, ::-1].ravel()

    def w(name):
        return g[name]

    w_sq = np.stack([
        np.concatenate([w("attn_Wd_q_w"), w("attn_Wd_kv_w")], axis=1),
        w("attn_Wk_r_w"), w("attn_Wk_r_w")[:, swap], w("attn_Wo_w"),
        w("ffn_W_r").T, w("ffn_W_k").T, w("ffn_W_v").T, np.eye(D, dtype=np.float32),
    ], axis=1)
    w_lat = np.stack([
        np.concatenate([w("attn_Wu_q_w"), w("attn_Wu_k_w")], axis=0),
        np.concatenate([w("attn_Wq_r_w"), w("attn_Wu_v_w")], axis=0),
        np.concatenate([w("attn_Wq_r_w")[:, swap], np.zeros((DL, D), np.float32)], axis=0),
    ], axis=1)
    cols = np.stack([
        np.concatenate([w("attn_Wd_q_b"), w("attn_Wd_kv_b")]),
        w("attn_Wu_q_b"), w("attn_Wq_r_b"), w("attn_Wq_r_b")[swap],
        w("attn_Wu_k_b"), w("attn_Wk_r_b"), w("attn_Wk_r_b")[swap],
        w("ffn_mu_r"), w("ffn_mu_k"),
    ], axis=1)
    rows = np.stack([np.broadcast_to(w("attn_Wu_v_b"), (P, D)), np.broadcast_to(w("attn_Wo_b"), (P, D))], axis=1)
    theta = (np.float32(10000.0) ** (np.float32(-2.0) * np.arange(D // 2, dtype=np.float32))
             / np.float32(D // 2)).astype(np.float32)
    angle = (np.arange(S, dtype=np.float32)[None, :] * np.repeat(theta, 2)[:, None]).astype(np.float32)
    sign = np.where(np.arange(D) % 2 == 0, -1.0, 1.0).astype(np.float32)[:, None]
    trig = np.stack([np.cos(angle), np.sin(angle) * sign], axis=1).astype(np.float32)

    arrays = {
        "x_dram": g["attn_x"], "w_sq_dram": w_sq, "w_lat_dram": w_lat, "cols_dram": cols,
        "rows_dram": rows, "trig_dram": trig, "ident_dram": np.eye(P).astype(ml_dtypes.bfloat16),
    }
    arrays = {k: np.ascontiguousarray(v) for k, v in arrays.items()}
    nc = bacc.Bacc("TRN2", target_bir_lowering=False, num_devices=1)
    args = [nc.dram_tensor(k, v.shape, mybir.dt.from_np(v.dtype), kind="ExternalInput").ap()
            for k, v in arrays.items()]
    out = nc.dram_tensor("out_dram", (B, S, D), F32, kind="ExternalOutput").ap()
    build(nc, *args, out)
    r = run_bass_kernel_spmd(nc, [arrays], core_ids=[0])
    return r.results[0]["out_dram"]
```

```python
from contextlib import ExitStack

import concourse.bass as bass
import numpy as np
from concourse import mybir

F32 = mybir.dt.float32
BF16 = mybir.dt.bfloat16
ACT = mybir.ActivationFunctionType
ALU = mybir.AluOpType
AX_X = mybir.AxisListType.X

P = 128
B, S, D = 8, 512, 128
H = 16
HD = D // H
DL = 64
T = S // P
UNITS = 4
HPU = H // UNITS
STEPS = 8
SPB = UNITS * STEPS
LEAD = 13
RUNS = ((0, 3), (1, 2), (2, 1))
PRODUCTS = sum(n for _, n in RUNS)
USED = PRODUCTS * HD
ROWS = 96
MAX_AT = ROWS
VW = 32
EPS = 1e-5
SCALE = 1.0 / float(H + DL + DL) ** 0.5
TWO_ONES = float(np.array([0x3F803F80], np.uint32).view(np.float32)[0])
DMA = 16

DOWN_T, KROPE, OUT, FFN_R, FFN_K, FFN_V, IDENT = range(7)
UP, QROPE = range(2)
UP_V = 1
TAIL_OUT, TAIL_SUM = range(2)
F_Q, F_QROPE, F_K, F_V = range(4)
B_DOWN, B_KR, B_UQ, B_QR, B_UK, B_UV, MU_R, MU_K, OMU_R, OMU_K = range(10)


ROOMY = SPB - LEAD + 3
STACKS = len(RUNS)
DCH = S * H // P
COLS_MAX = 3 * HPU * T


def build(nc, x, w_sq_dram, w_lat_dram, cols_dram, row_o_dram, trig_dram, ident_dram, w_tail_dram, out):
    x_view = x.rearrange("b (t p) c -> b p t c", p=P)
    out_view = out.rearrange("b (t p) c -> b p t c", p=P)

    with ExitStack() as ctx:
        def sb(name, shape, dt=F32):
            return ctx.enter_context(nc.sbuf_tensor(name, shape, dt))

        def psum(name, shape, dt=F32):
            return ctx.enter_context(nc.psum_tensor(name, shape, dt))

        def sem(name):
            return ctx.enter_context(nc.semaphore(name))

        w_sq = sb("w_sq", [P, 7, P])
        w_lat = sb("w_lat", [P, 2, P])
        w_fold = sb("w_fold", [P, 4, P])
        cols = sb("cols", [P, 10])
        b_fold = sb("b_fold", [P, 4])
        bv_wide = sb("bv_wide", [P, P])
        row_o = sb("row_o", [P, P])
        row_sum = sb("row_sum", [P, P])
        trig = sb("trig", [P, 2, S])
        w_tail = sb("w_tail", [P, 2, P])
        ident_bf = sb("ident_bf", [P, P], BF16)
        half = sb("half", [P, T])
        x_in = [sb(f"x_in{i}", [P, T, D]) for i in range(2)]
        stats = sb("stats", [P, T, 6])
        mean_var = sb("mean_var", [P, T, 2])
        var_eps = sb("var_eps", [P, T])
        rstd = sb("rstd", [P, T])
        xn = sb("xn", [P, T, D])
        xT = sb("xT", [P, 1 + S])
        pre = {n: sb(f"{n}_pre", [P, S]) for n in "qk"}
        swapped = {n: sb(f"{n}_swapped", [P, S]) for n in "qk"}
        rot_c = {n: sb(f"{n}_rot_c", [P, S]) for n in "qk"}
        rot_s = {n: sb(f"{n}_rot_s", [P, S]) for n in "qk"}
        rot = {n: sb(f"{n}_rot", [P, S]) for n in "qk"}
        full = {n: sb(f"{n}_full", [P, S]) for n in "qk"}
        rest = {n: sb(f"{n}_rest", [P, S]) for n in "qk"}
        parts = {n: sb(f"{n}_parts", [P, 3, S], BF16) for n in "qk"}
        q_stack = [sb(f"q_stack{i}", [P, H, S], BF16) for i in range(2)]
        k_stack = [sb(f"k_stack{i}", [P, H, S], BF16) for i in range(2)]
        vals = [sb(f"vals{i}", [P, T, H, VW]) for i in range(2)]
        probs = sb("probs", [P, STEPS, 2, S])
        neg_max = [sb(f"neg_max{i}", [P, HPU * T]) for i in range(2)]
        max_rest = sb("max_rest", [P, HPU * T])
        max_cols = sb("max_cols", [P, P], BF16)
        max_parts = max_cols[:, 0:COLS_MAX].rearrange("p (k c) -> p k c", k=3)
        zeros = sb("zeros", [P, HPU * T])
        max_rows = [sb(f"max_rows{i}", [COLS_MAX, P], BF16) for i in range(2)]
        pv = [sb(f"pv{i}", [P, S]) for i in range(2)]
        num = sb("num", [P, S])
        den = sb("den", [P, DCH])
        rden_c = sb("rden_c", [P, DCH])
        rden = sb("rden", [P, S])
        attnT = sb("attnT", [P, S])
        tail_rden, tail_attn = rot_c["q"], rot_c["k"]
        mix_a = {n: sb(f"mix_a_{n}", [P, S]) for n in "rk"}
        mix_b = {n: sb(f"mix_b_{n}", [P, S]) for n in "rk"}
        mixed = {n: sb(f"mixed_{n}", [P, S]) for n in "rk"}
        gate = sb("gate", [P, T, D])
        relu = sb("relu", [P, S])
        relu_sq = sb("relu_sq", [P, S])
        gated = sb("gated", [P, T, D])
        x_bias = sb("x_bias", [P, T, D])
        base = [sb(f"base{i}", [P, T, D]) for i in range(2)]
        y = sb("y", [P, T, D])

        ps_max = [psum(f"ps_max{i}", [P, 2, S]) for i in range(2)]
        ps_exp = [psum(f"ps_exp{g}", [P, S]) for g in range(2)]
        ps_pv = psum("ps_pv", [P, S])
        ps_misc = psum("ps_misc", [P, S])
        ps_tail_sum = ps_max[0][:, 0, :]
        ps_misc_bf = ps_misc[:, :].bitcast(BF16)
        first_bank = {
            "xT": ps_misc[:, :], "k_rope": ps_exp[0][:, :], "q_rope": ps_exp[1][:, :],
            "k_lin": ps_max[0][:, 0, :], "q_lin": ps_max[0][:, 1, :], "vals": ps_pv[:, :],
            "ffn_r": ps_misc[:, :], "ffn_k": ps_exp[0][:, :],
        }
        ps_fold = ps_max[1][:, :, 0:2 * P]
        ps_bias = ps_max[0][:, :, 0:2]
        ps_row = ps_max[1][:, 0, 0:P]

        HALVES = ((0, T // 2), (T // 2, T))
        WHOLE = (0, T)
        OTHERS = (UNITS - 1) * HPU * HD

        def roomy(b, s):
            return isinstance(b, int) and b == B - 1 and s > ROOMY

        def exp_bank(b, s, g):
            return ps_max[1][:, g, :] if roomy(b, s) and s % 2 == 1 else ps_exp[g][:, :]

        def bank(job, n):
            return first_bank[job] if job in first_bank and isinstance(n, int) and n == 0 else ps_misc[:, :]

        def tok(job, n):
            return bank(job, n).rearrange("p (t c) -> p t c", t=T)

        spills = {n: nc.dram_tensor(f"{n}_spill", (3, HD, H, S), BF16, kind="Internal").ap() for n in "qk"}
        pv_spill = nc.dram_tensor("pv_spill", (UNITS, HPU, VW, S), F32, kind="Internal").ap()
        rden_spill = nc.dram_tensor("rden_spill", (H, S), F32, kind="Internal").ap()

        ident_in = sem("ident_in")
        consts_in = sem("consts_in")
        trig_in = sem("trig_in")
        row_in = sem("row_in")
        ident_bf_in = sem("ident_bf_in")
        w_tail_in = sem("w_tail_in")
        tail_sum_ready = sem("tail_sum_ready")
        tail_rden_ready = sem("tail_rden_ready")
        tail_attn_ready = sem("tail_attn_ready")
        edge_filled = sem("edge_filled")
        vals_filled = sem("vals_filled")
        cleared = sem("cleared")
        halved = sem("halved")
        bv_ready = sem("bv_ready")
        omu_ready = sem("omu_ready")
        x_landed = sem("x_landed")
        stats_ready = sem("stats_ready")
        mv_ready = sem("mv_ready")
        var_ready = sem("var_ready")
        rstd_ready = sem("rstd_ready")
        xn_ready = sem("xn_ready")
        JOBS = ("xT", "k_rope", "q_rope", "vals", "k_lin", "q_lin", "fold", "bias", "row",
                "ffn_r", "ffn_k", "ffn_v", "out", "max")
        ready = {n: sem(f"{n}_ready") for n in JOBS}
        taken = {n: sem(f"{n}_taken") for n in JOBS}
        swap_in = {n: sem(f"{n}_swap_in") for n in "qk"}
        cos_ready = {n: sem(f"{n}_cos_ready") for n in "qk"}
        sin_ready = {n: sem(f"{n}_sin_ready") for n in "qk"}
        rot_ready = {n: sem(f"{n}_rot_ready") for n in "qk"}
        part0_ready = {n: sem(f"{n}_part0_ready") for n in "qk"}
        rest_ready = {n: sem(f"{n}_rest_ready") for n in "qk"}
        part1_ready = {n: sem(f"{n}_part1_ready") for n in "qk"}
        part2_ready = {n: sem(f"{n}_part2_ready") for n in "qk"}
        spilled = {n: sem(f"{n}_spilled") for n in "qk"}
        stacked = {n: sem(f"{n}_stacked") for n in "qk"}
        mix_half = sem("mix_half")
        mixed_ready = {n: sem(f"mixed_{n}_ready") for n in "rk"}
        relu_sq_ready = sem("relu_sq_ready")
        x_bias_ready = sem("x_bias_ready")
        base_ready = sem("base_ready")
        raw_scores = sem("raw_scores")
        row_max = sem("row_max")
        max_split = sem("max_split")
        max_parts_ready = sem("max_parts_ready")
        max_stacked = [sem(f"max_stacked{i}") for i in range(2)]
        scores_ready = [sem(f"scores_ready{g}") for g in range(2)]
        probs_ready = [sem(f"probs_ready{g}") for g in range(2)]
        pv_done = sem("pv_done")
        pv_taken = sem("pv_taken")
        pv_spilled = [sem(f"pv_spilled{i}") for i in range(2)]
        pv_gathered = sem("pv_gathered")
        rden_ready = sem("rden_ready")
        rden_spilled = sem("rden_spilled")
        rden_spread = sem("rden_spread")
        attn_ready = sem("attn_ready")
        stored = sem("stored")

        block = ctx.enter_context(nc.Block())


        def batches(eng, body):
            body(0, 0)
            with eng.Fori(0, (B - 2) // 2) as i:
                body(2 * i + 1, 1)
                body(2 * i + 2, 0)
            body(B - 1, 1)
            body(B, 0)

        def steps(b, par):
            for o in range(STEPS if ended(b) else SPB):
                if o >= STEPS:
                    yield o, b, par, o - STEPS
                else:
                    yield o, b - 1, 1 - par, o + SPB - STEPS

        def softmax_begun(c):
            return not (isinstance(c, int) and c < 0)

        def ended(b):
            return isinstance(b, int) and b == B

        def first(b):
            return isinstance(b, int) and b == 0

        def last(b):
            return isinstance(b, int) and b >= B - 1

        def sin_half(q, isa, name, n):
            q.wait_ge(swap_in[name], 2 * DMA * (n + 1))
            isa.tensor_tensor(rot_s[name][:, :], swapped[name][:, :], trig[:, 1, :],
                              ALU.mult).then_inc(sin_ready[name], 1)

        def add_halves(q, isa, name, n):
            q.wait_ge(cos_ready[name], n + 1)
            q.wait_ge(sin_ready[name], n + 1)
            if not (isinstance(n, int) and n == 0):
                q.wait_ge(taken[f"{name}_lin"], n)
            isa.tensor_tensor(rot[name][:, :], rot_c[name][:, :], rot_s[name][:, :],
                              ALU.add).then_inc(rot_ready[name], 1)

        def rest_after_part0(q, isa, name, n):
            q.wait_ge(part0_ready[name], n + 1)
            isa.tensor_tensor(rest[name][:, :], full[name][:, :], parts[name][:, 0, :],
                              ALU.subtract).then_inc(rest_ready[name], 1)

        def part2(q, isa, name, n):
            q.wait_ge(part1_ready[name], n + 1)
            isa.tensor_tensor(parts[name][:, 2, :], rest[name][:, :], parts[name][:, 1, :],
                              ALU.subtract).then_inc(part2_ready[name], 1)

        @block.sync
        def _(sp):
            def value(count):
                if not isinstance(count, int):
                    sp.compute_val(count)
                return count

            def load_x(n, par):
                sp.dma_start(x_in[par][:, :, :], x_view[n]).then_inc(x_landed, DMA)

            def swap(name, n):
                halves_read = value(n)
                sp.wait_ge(taken[f"{name}_rope"], n + 1)
                if not (isinstance(n, int) and n == 0):
                    sp.wait_ge(rot_ready[name], halves_read)
                for side in range(2):
                    sp.dma_start(swapped[name][side:P:2, :], pre[name][1 - side:P:2, :]).then_inc(swap_in[name], DMA)

            def spill_part(name, part):
                sp.dma_start(spills[name][part].rearrange("d h q -> h d q"),
                             parts[name][:, part, :]).then_inc(spilled[name], DMA)

            def spill(name, n):
                copies_read = value(STACKS * DMA * n)
                sp.wait_ge(part2_ready[name], n + 1)
                if not (isinstance(n, int) and n == 0):
                    sp.wait_ge(stacked[name], copies_read)
                for part in range(3):
                    spill_part(name, part)

            def stack(name, n, par):
                scores_read = value(SPB * (n - 1))
                sp.wait_ge(spilled[name], 3 * DMA * (n + 1))
                if not (isinstance(n, int) and n < 2):
                    sp.wait_ge(scores_ready[1], scores_read)
                dst = (q_stack if name == "q" else k_stack)[par]
                at = 0
                for q_part, count in RUNS:
                    if name == "q":
                        src = spills[name][q_part:q_part + 1].to_broadcast([count, HD, H, S])
                    else:
                        src = spills[name][0:count]
                    sp.dma_start(dst[at:at + HD * count, :, :], src).then_inc(stacked[name], DMA)
                    at += HD * count

            def stack_max(unit, u, par, x_read=None):
                sp.wait_ge(taken["max"], unit + 1)
                if x_read is not None:
                    sp.wait_ge(x_bias_ready, x_read)
                sp.dma_start(q_stack[par][MAX_AT:MAX_AT + 3, HPU * u:HPU * (u + 1), :],
                             max_rows[u % 2][:, :]).then_inc(max_stacked[u % 2], DMA)

            def spill_pv(b, u):
                sp.wait_ge(pv_taken, UNITS * b + u + 1)
                if u == 0 and not first(b):
                    sp.wait_ge(pv_gathered, 2 * DMA * b)
                sp.dma_start(pv_spill[u].rearrange("j r q -> (j r) q"),
                             pv[u % 2][:, :]).then_inc(pv_spilled[u % 2], DMA)

            def gather(b, units=UNITS):
                sp.wait_ge(pv_spilled[0], UNITS // 2 * DMA * (b + 1))
                if units == UNITS:
                    sp.wait_ge(pv_spilled[1], UNITS // 2 * DMA * (b + 1))
                else:
                    sp.wait_ge(pv_spilled[1], UNITS // 2 * DMA * (b + 1) - DMA)
                heads = units * HPU
                strips = pv_spill[0:units].rearrange("u j r q -> (u j) r q")
                sp.dma_start(num[0:heads * HD, :], strips[:, 0:HD, :]).then_inc(pv_gathered, DMA)
                sp.dma_start(den[0:heads * HD, :],
                             strips[:, HD:HD + 1, :].rearrange("h o (k q) -> h (o k) q", q=DCH)
                             ).then_inc(pv_gathered, DMA)

            def spread_inverse(b, heads=H):
                sp.wait_ge(rden_ready, b + 1)
                sp.dma_start(rden_spill[0:heads].rearrange("h (k q) -> (h k) q", q=DCH),
                             rden_c[0:heads * HD, :]).then_inc(rden_spilled, DMA)
                sp.wait_ge(rden_spilled, DMA * (b + 1))
                src = rden_spill[0:heads].rearrange("(h o) q -> h o q", o=1).to_broadcast([heads, HD, S])
                sp.dma_start(rden[0:heads * HD, :], src).then_inc(rden_spread, DMA)

            def store(b):
                sp.wait_ge(taken["out"], b + 1)
                sp.dma_start(out_view[b], y[:, :, :]).then_inc(stored, DMA)

            def body(b, par):
                for o, c, cpar, s in steps(b, par):
                    more = not last(b)
                    if o == 0 and more:
                        load_x(b + 1, 1 - par)
                    if o % STEPS == 3 and softmax_begun(c) and s >= STEPS:
                        spill_pv(c, s // STEPS - 1)
                    elif o == 11 and not first(b):
                        spill_pv(b - 1, UNITS - 1)
                    if o % STEPS == 5 and not ended(b):
                        stack_max(UNITS * b + o // STEPS, o // STEPS, par,
                                  x_read=b + 1 if o == 29 else None)
                    if more:
                        if o == 9:
                            swap("k", b + 1)
                        if o == 11:
                            swap("q", b + 1)
                        if o == 18:
                            spill("k", b + 1)
                        if o == 20:
                            spill("q", b + 1)
                        if o == 21:
                            stack("k", b + 1, 1 - par)
                            stack("q", b + 1, 1 - par)
                    if not first(b) and not ended(b):
                        if o == 11:
                            gather(b - 1)
                        if o == 15:
                            spread_inverse(b - 1)
                        if o == 29:
                            store(b - 1)

            sp.dma_start(x_in[0][:, :, :], x_view[0]).then_inc(x_landed, DMA)
            sp.dma_start(w_sq[:, IDENT, :], w_sq_dram[:, IDENT, :]).then_inc(ident_in, DMA)
            sp.dma_start(w_sq[:, 0:IDENT, :], w_sq_dram[:, 0:IDENT, :]).then_inc(consts_in, DMA)
            sp.dma_start(w_lat[:, :, :], w_lat_dram).then_inc(consts_in, DMA)
            sp.dma_start(cols[:, 0:OMU_R], cols_dram).then_inc(consts_in, DMA)
            sp.dma_start(trig[:, :, :], trig_dram).then_inc(trig_in, DMA)
            sp.dma_start(row_o[:, :], row_o_dram).then_inc(row_in, DMA)
            sp.dma_start(ident_bf[:, :], ident_dram).then_inc(ident_bf_in, DMA)
            sp.dma_start(w_tail[:, :, :], w_tail_dram).then_inc(w_tail_in, DMA)
            swap("k", 0)
            swap("q", 0)
            sp.wait_ge(cleared, 4)
            for name in "kq":
                for part, done in enumerate((part0_ready, part1_ready, part2_ready)):
                    sp.wait_ge(done[name], 1)
                    spill_part(name, part)
            for name in "kq":
                stack(name, 0, 0)
            batches(sp, body)
            gather(B - 1, UNITS - 1)
            spread_inverse(B - 1, (UNITS - 1) * HPU)
            store(B - 1)
            sp.wait_ge(stored, DMA * (B + 1))

        CONSTS = 3 * DMA

        @block.tensor
        def _(pe):
            mm = nc.tensor.matmul

            def project(job, n, w, rhs, tiles=WHOLE):
                at = slice(tiles[0] * P, tiles[1] * P)
                last_mm = mm(bank(job, n)[:, at], w, rhs[:, at], start=True, stop=True)
                if tiles[1] == T:
                    last_mm.then_inc(ready[job], 1)

            def project_tokens(job, n, lhs, w, tiles=WHOLE):
                for t in range(*tiles):
                    last_mm = mm(tok(job, n)[:, t, :], lhs[:, t * P:(t + 1) * P], w, start=True, stop=True)
                if tiles[1] == T:
                    last_mm.then_inc(ready[job], 1)

            def bank_free(job_before, n):
                if not (isinstance(n, int) and n == 0):
                    pe.wait_ge(taken[job_before], n + 1)

            def transpose_x(n):
                pe.wait_ge(xn_ready, n + 1)
                if not (isinstance(n, int) and n == 0):
                    pe.wait_ge(taken["max"], UNITS * (n - 1) + 1)
                for t in range(T):
                    last_mm = nc.tensor.transpose(tok("xT", n)[:, t, :], xn[:, t, :], w_sq[:, IDENT, :])
                last_mm.then_inc(ready["xT"], 1)

            def k_rope(n):
                pe.wait_ge(taken["xT"], n + 1)
                project("k_rope", n, w_sq[:, KROPE, :], xT[:, 1:1 + S])

            def q_rope(n):
                bank_free("k_rope", n)
                project("q_rope", n, w_fold[:, F_QROPE, :], xT[:, 1:1 + S])

            def values(n):
                bank_free("q_lin", n)
                project_tokens("vals", n, xT[:, 1:1 + S], w_fold[:, F_V, :])

            def k_lin(n):
                bank_free("q_rope", n)
                project("k_lin", n, w_fold[:, F_K, :], xT[:, 1:1 + S])

            def q_lin(n):
                if not (isinstance(n, int) and n == 0):
                    pe.wait_ge(taken["max"], UNITS * (n - 1) + 2)
                project("q_lin", n, w_fold[:, F_Q, :], xT[:, 1:1 + S])

            def ffn_r(n, tiles=WHOLE):
                if tiles[0] == 0:
                    bank_free("vals", n)
                    pe.wait_ge(mixed_ready["r"], n + 1)
                project_tokens("ffn_r", n, mixed["r"][:, :], w_sq[:, FFN_R, :], tiles)

            def ffn_k(n, tiles=WHOLE, maxima_taken=None):
                if tiles[0] == 0:
                    if maxima_taken is not None:
                        pe.wait_ge(taken["max"], maxima_taken)
                    pe.wait_ge(mixed_ready["k"], n + 1)
                project("ffn_k", n, w_sq[:, FFN_K, :], mixed["k"][:, :], tiles)

            def ffn_v(n, tiles):
                if tiles[0] == 0:
                    if not (isinstance(n, int) and n == 0):
                        pe.wait_ge(taken["max"], UNITS * n)
                    pe.wait_ge(relu_sq_ready, n + 1)
                project_tokens("ffn_v", n, relu_sq[:, :], w_sq[:, FFN_V, :], tiles)

            def transpose_max(unit, before):
                pe.wait_ge(*before)
                pe.wait_ge(max_parts_ready, unit + 1)
                nc.tensor.transpose(ps_misc_bf[:, 0:P], max_cols[:, :], ident_bf[:, :]).then_inc(ready["max"], 1)

            def out_projection(b, tiles=WHOLE, before=None):
                if tiles[0] == 0:
                    pe.wait_ge(*before)
                    pe.wait_ge(attn_ready, b + 1)
                project_tokens("out", b, attnT[:, :], w_sq[:, OUT, :], tiles)

            def scores_for_max(b, par, r):
                if r == 0:
                    pe.wait_ge(stacked["k"], STACKS * DMA * (b + 1))
                    pe.wait_ge(stacked["q"], STACKS * DMA * (b + 1))
                if not (first(b) and r < 2):
                    pe.wait_ge(row_max, SPB * b + r - 1)
                for g in range(2):
                    head, qt = 2 * (r // T) + g, r % T
                    last_mm = mm(ps_max[r % 2][:, g, :], q_stack[par][0:ROWS, head, qt * P:(qt + 1) * P],
                                 k_stack[par][0:ROWS, head, :], start=True, stop=True)
                last_mm.then_inc(raw_scores, 1)

            def scores_for_exp(b, par, s, g):
                u, kt, pp = s // STEPS, s % STEPS // 2, s % 2
                if s % STEPS == 0 and g == 0:
                    pe.wait_ge(max_stacked[u % 2], DMA * (UNITS // 2 * b + u // 2 + 1))
                if roomy(b, s):
                    pe.wait_ge(probs_ready[g], SPB * b + s - 1)
                elif not (first(b) and s < 1):
                    pe.wait_ge(probs_ready[g], SPB * b + s)
                if roomy(b, s) and s == ROOMY + 1:
                    pe.wait_ge(row_max, B * SPB)
                head = HPU * u + 2 * pp + g
                mm(exp_bank(b, s, g), k_stack[par][:, head, kt * P:(kt + 1) * P],
                   q_stack[par][:, head, :], start=True, stop=True).then_inc(scores_ready[g], 1)

            def probs_values(b, par, u, kt, tiles=WHOLE):
                at = slice(tiles[0] * P, tiles[1] * P)
                pe.wait_ge(probs_ready[1], SPB * b + STEPS * u + 2 * kt + 2)
                if kt == 0 and not (first(b) and u == 0):
                    pe.wait_ge(pv_taken, UNITS * b + u)
                for j in range(HPU):
                    last_mm = mm(ps_pv[VW * j:VW * (j + 1), at], vals[par][:, kt, HPU * u + j, :],
                                 probs[:, 2 * kt + j // 2, j % 2, at], start=kt == 0, stop=kt == T - 1)
                if tiles[1] == T:
                    last_mm.then_inc(pv_done, 1)

            def ahead(b, par, s):
                r = s + LEAD
                if r < SPB:
                    scores_for_max(b, par, r)
                elif not last(b):
                    scores_for_max(b + 1, 1 - par, r - SPB)

            def body(b, par):
                n, more = b + 1, not last(b)
                for o, c, cpar, s in steps(b, par):
                    if softmax_begun(c):
                        scores_for_exp(c, cpar, s, 0)
                    ahead(c, cpar, s)
                    if softmax_begun(c):
                        scores_for_exp(c, cpar, s, 1)
                        u = s // STEPS
                        if o in IDLE and not ended(b):
                            probs_values(c, cpar, u, (s % STEPS - 2) // 2, HALVES[0])
                        elif s % STEPS in (3, 5, 7):
                            probs_values(c, cpar, u, (s % STEPS - 3) // 2,
                                         HALVES[1] if o - 1 in IDLE and not ended(b) else WHOLE)
                        elif s % STEPS == 1 and s > 1:
                            probs_values(c, cpar, u - 1, T - 1)
                        elif s == 1 and not first(c):
                            probs_values(c - 1, 1 - cpar, UNITS - 1, T - 1)
                    if not ended(b):
                        jobs(b, n, more, o)
                        maxima(b, n, more, o)

            def maxima(b, n, more, o):
                if o == 5:
                    transpose_max(UNITS * b, (taken["ffn_v"], b + 1))
                if o == 13:
                    transpose_max(UNITS * b + 1, (taken["k_lin"], n + 1) if more
                                  else (taken["max"], UNITS * b + 1))
                if o == 21:
                    transpose_max(UNITS * b + 2, (taken["ffn_r"], n + 1) if more
                                  else (taken["max"], UNITS * b + 2))
                if o == 29:
                    transpose_max(UNITS * b + 3, (taken["ffn_k"], n + 1) if first(b) else (taken["out"], b))

            IDLE = (4, 30)

            def jobs(b, n, more, o):
                if o in (0, 2):
                    ffn_v(b, HALVES[o // 2])
                if more:
                    if o == 6:
                        transpose_x(n)
                    if o == 8:
                        k_rope(n)
                    if o == 10:
                        q_rope(n)
                    if o == 12:
                        k_lin(n)
                    if o == 14:
                        q_lin(n)
                    if o == 16:
                        values(n)
                    if o in (18, 20):
                        ffn_r(n, HALVES[(o - 18) // 2])
                    if o in (22, 24):
                        ffn_k(n, HALVES[(o - 22) // 2], UNITS * b + 3)
                if o in (26, 28) and not first(b):
                    out_projection(b - 1, HALVES[(o - 26) // 2],
                                   (taken["ffn_k"], n + 1) if more else (taken["max"], UNITS * b + 3))

            pe.wait_ge(consts_in, CONSTS)
            for half, at in enumerate((0, DL)):
                last_mm = mm(ps_fold[:, half, :], w_sq[at:at + DL, DOWN_T, :],
                             w_lat[at:at + DL, :, :], start=True, stop=True)
            last_mm.then_inc(ready["fold"], 1)
            pe.wait_ge(ident_in, DMA)
            transpose_x(0)
            k_rope(0)
            pe.wait_ge(taken["fold"], 1)
            q_rope(0)
            for half, at in enumerate((0, DL)):
                for which in range(2):
                    last_mm = mm(ps_bias[:, half, which:which + 1], w_lat[at:at + DL, which, :],
                                 cols[at:at + DL, B_DOWN:B_DOWN + 1], start=True, stop=True)
            last_mm.then_inc(ready["bias"], 1)
            pe.wait_ge(taken["bias"], 1)
            k_lin(0)
            q_lin(0)
            values(0)
            pe.wait_ge(bv_ready, 1)
            mm(ps_row, bv_wide[:, :], w_sq[:, OUT, :], start=True, stop=True).then_inc(ready["row"], 1)
            ffn_r(0)
            pe.wait_ge(taken["k_rope"], 1)
            ffn_k(0)
            pe.wait_ge(taken["row"], 1)
            for r in range(LEAD - STEPS):
                scores_for_max(0, 0, r)
            pe.wait_ge(halved, 1)
            pe.wait_ge(ident_bf_in, DMA)
            batches(pe, body)
            probs_values(B - 1, 1, UNITS - 1, T - 1)
            pe.wait_ge(w_tail_in, DMA)
            pe.wait_ge(pv_taken, UNITS * B)
            mm(ps_tail_sum, w_tail[:, TAIL_SUM, :], pv[(UNITS - 1) % 2][:, :],
               start=True, stop=True).then_inc(tail_sum_ready, 1)
            pe.wait_ge(taken["max"], UNITS * B)
            pe.wait_ge(attn_ready, B)
            for part, tiles in enumerate(HALVES):
                pe.wait_ge(tail_attn_ready, part + 1)
                for t in range(*tiles):
                    mm(ps_misc[:, t * P:(t + 1) * P], attnT[0:OTHERS, t * P:(t + 1) * P],
                       w_sq[0:OTHERS, OUT, :], start=True, stop=False)
                    last_mm = mm(ps_misc[:, t * P:(t + 1) * P], tail_attn[:, t * P:(t + 1) * P],
                                 w_tail[:, TAIL_OUT, :], start=False, stop=True)
            last_mm.then_inc(ready["out"], 1)

        @block.scalar
        def _(act):
            activation = nc.scalar.activation

            def take_xT(n):
                act.wait_ge(ready["xT"], n + 1)
                if not (isinstance(n, int) and n == 0):
                    act.wait_ge(ready["vals"], n)
                    act.wait_ge(mixed_ready["k"], n)
                activation(xT[:, 1:1 + S], bank("xT", n), ACT.Copy).then_inc(taken["xT"], 1)

            def take_rope(name, n):
                act.wait_ge(ready[f"{name}_rope"], n + 1)
                if not (isinstance(n, int) and n == 0):
                    act.wait_ge(rot_ready[name], n)
                bias = cols[:, B_KR:B_KR + 1] if name == "k" else b_fold[:, F_QROPE:F_QROPE + 1]
                activation(pre[name][:, :], bank(f"{name}_rope", n), ACT.Identity,
                           bias=bias).then_inc(taken[f"{name}_rope"], 1)

            def take_values(n, par):
                act.wait_ge(ready["vals"], n + 1)
                if not (isinstance(n, int) and n < 2):
                    act.wait_ge(pv_done, T * UNITS * (n - 1))
                activation(vals[par][:, :, :, :].rearrange("p t h c -> p (t h) c")[:, :, 0:HD],
                           bank("vals", n).rearrange("p (h d) -> p h d", d=HD), ACT.Copy).then_inc(taken["vals"], 1)

            def part0(name, n):
                act.wait_ge(taken[f"{name}_lin"], n + 1)
                if not (isinstance(n, int) and n == 0):
                    act.wait_ge(stacked[name], STACKS * DMA * n)
                activation(parts[name][:, 0, :], full[name][:, :], ACT.Copy).then_inc(part0_ready[name], 1)

            def part1(name, n):
                act.wait_ge(rest_ready[name], n + 1)
                activation(parts[name][:, 1, :], rest[name][:, :], ACT.Copy).then_inc(part1_ready[name], 1)

            def take_max(b, u):
                act.wait_ge(ready["max"], UNITS * b + u + 1)
                if not (first(b) and u < 2):
                    act.wait_ge(max_stacked[u % 2], DMA * (UNITS // 2 * b + u // 2))
                activation(max_rows[u % 2][:, :], ps_misc_bf[0:COLS_MAX, 0:P], ACT.Copy).then_inc(taken["max"], 1)

            def take_ffn_r(n):
                act.wait_ge(ready["ffn_r"], n + 1)
                if not (isinstance(n, int) and n == 0):
                    act.wait_ge(taken["ffn_v"], n)
                activation(gate[:, :, :], tok("ffn_r", n), ACT.Tanh, scale=0.5).then_inc(taken["ffn_r"], 1)

            def take_ffn_k(n):
                act.wait_ge(ready["ffn_k"], n + 1)
                if not (isinstance(n, int) and n == 0):
                    act.wait_ge(relu_sq_ready, n)
                activation(relu[:, :], bank("ffn_k", n), ACT.Relu).then_inc(taken["ffn_k"], 1)

            def softmax_exp(b, s):
                for g in range(2):
                    act.wait_ge(scores_ready[g], SPB * b + s + 1)
                    if g == 0 and not (first(b) and s < STEPS):
                        act.wait_ge(pv_done, T * (UNITS * b + s // STEPS - 1) + s % STEPS // 2 + 1)
                    activation(probs[:, s % STEPS, g, :], exp_bank(b, s, g), ACT.Exp,
                               scale=SCALE).then_inc(probs_ready[g], 1)

            def take_pv(b, u):
                act.wait_ge(pv_done, T * (UNITS * b + u + 1))
                if not (first(b) and u < 2):
                    act.wait_ge(pv_spilled[u % 2], DMA * (UNITS // 2 * b + u // 2))
                activation(pv[u % 2][:, :], ps_pv[:, :], ACT.Copy).then_inc(pv_taken, 1)

            def body(b, par):
                n, more = b + 1, not last(b)
                for o, c, cpar, s in steps(b, par):
                    if softmax_begun(c):
                        if s % STEPS == 2 and s > 2:
                            take_pv(c, s // STEPS - 1)
                        elif s == 2 and not first(c):
                            take_pv(c - 1, UNITS - 1)
                        softmax_exp(c, s)
                    if o % STEPS == 5 and not ended(b):
                        take_max(b, o // STEPS)
                    if more:
                        if o == 6:
                            take_xT(n)
                        if o == 8:
                            take_rope("k", n)
                        if o == 10:
                            take_rope("q", n)
                        if o == 13:
                            part0("k", n)
                        if o == 15:
                            part0("q", n)
                        if o == 16:
                            part1("k", n)
                            take_values(n, 1 - par)
                        if o == 18:
                            part1("q", n)
                        if o == 20:
                            take_ffn_r(n)
                        if o == 24:
                            take_ffn_k(n)

            act.wait_ge(ready["fold"], 1)
            activation(w_fold[:, :, :].rearrange("p (h k) c -> p h (k c)", h=2), ps_fold,
                       ACT.Copy).then_inc(taken["fold"], 1)
            act.wait_ge(edge_filled, 1)
            take_xT(0)
            act.wait_ge(consts_in, CONSTS)
            take_rope("k", 0)
            act.wait_ge(taken["bias"], 1)
            take_rope("q", 0)
            act.wait_ge(vals_filled, 1)
            take_values(0, 0)
            part0("k", 0)
            part1("k", 0)
            part0("q", 0)
            part1("q", 0)
            take_ffn_r(0)
            take_ffn_k(0)
            batches(act, body)
            take_pv(B - 1, UNITS - 1)

        @block.vector
        def _(dve):
            vec = nc.vector

            def layer_norm_stats(n, par):
                dve.wait_ge(x_landed, DMA * (n + 1))
                for t in range(T):
                    last_op = vec.bn_stats(stats[:, t, :], x_in[par][:, t, :])
                last_op.then_inc(stats_ready, 1)

            def mean_variance(n):
                for t in range(T):
                    last_op = vec.bn_aggr(mean_var[:, t, :], stats[:, t, :])
                last_op.then_inc(mv_ready, 1)
                dve.wait_ge(mv_ready, n + 1)
                vec.tensor_scalar(var_eps[:, :], mean_var[:, :, 1], EPS, None, ALU.add).then_inc(var_ready, 1)

            def layer_norm(n, par):
                dve.wait_ge(rstd_ready, n + 1)
                if not (isinstance(n, int) and n == 0):
                    dve.wait_ge(ready["xT"], n)
                for t in range(T):
                    last_op = vec.tensor_scalar(xn[:, t, :], x_in[par][:, t, :], mean_var[:, t, 0:1],
                                                rstd[:, t:t + 1], ALU.subtract, ALU.mult)
                last_op.then_inc(xn_ready, 1)

            def cos_half(name, n):
                dve.wait_ge(taken[f"{name}_rope"], n + 1)
                if not (isinstance(n, int) and n == 0):
                    dve.wait_ge(rot_ready[name], n)
                vec.tensor_tensor(rot_c[name][:, :], pre[name][:, :], trig[:, 0, :],
                                  ALU.mult).then_inc(cos_ready[name], 1)

            def add_linear(name, n):
                dve.wait_ge(ready[f"{name}_lin"], n + 1)
                dve.wait_ge(rot_ready[name], n + 1)
                if not (isinstance(n, int) and n == 0):
                    dve.wait_ge(rest_ready[name], n)
                bias = F_Q if name == "q" else F_K
                vec.scalar_tensor_tensor(full[name][:, :], bank(f"{name}_lin", n), b_fold[:, bias:bias + 1],
                                         rot[name][:, :], ALU.add, ALU.add).then_inc(taken[f"{name}_lin"], 1)

            def take_ffn_v(n):
                dve.wait_ge(ready["ffn_v"], n + 1)
                dve.wait_ge(taken["ffn_r"], n + 1)
                if not (isinstance(n, int) and n == 0):
                    dve.wait_ge(base_ready, n)
                vec.scalar_tensor_tensor(gated[:, :, :], gate[:, :, :], 1.0, tok("ffn_v", n),
                                         ALU.add, ALU.mult).then_inc(taken["ffn_v"], 1)

            def invert(b, rows=P):
                dve.wait_ge(pv_gathered, 2 * DMA * (b + 1))
                vec.reciprocal(rden_c[0:rows, :], den[0:rows, :]).then_inc(rden_ready, 1)

            def normalise(b, rows=P):
                dve.wait_ge(rden_spread, DMA * (b + 1))
                vec.tensor_tensor(attnT[0:rows, :], num[0:rows, :], rden[0:rows, :],
                                  ALU.mult).then_inc(attn_ready, 1)

            def normalise_tail(part):
                at = slice(HALVES[part][0] * P, HALVES[part][1] * P)
                vec.reciprocal(tail_rden[:, at], ps_tail_sum[:, at]).then_inc(tail_rden_ready, 1)
                dve.wait_ge(tail_rden_ready, part + 1)
                vec.tensor_tensor(tail_attn[:, at], pv[(UNITS - 1) % 2][:, at], tail_rden[:, at],
                                  ALU.mult).then_inc(tail_attn_ready, 1)

            def finish(b, par):
                dve.wait_ge(ready["out"], b + 1)
                dve.wait_ge(base_ready, b + 1)
                dve.wait_ge(stored, DMA * (b + 1))
                vec.tensor_tensor(y[:, :, :], tok("out", b), base[par][:, :, :], ALU.add).then_inc(taken["out"], 1)

            def reduce_rows(b, r):
                unit, c = r // STEPS, r % STEPS
                dve.wait_ge(raw_scores, SPB * b + r + 1)
                if c == 0 and not (first(b) and unit < 2):
                    dve.wait_ge(max_parts_ready, UNITS * b + unit - 1)
                pair, qt = c // T, c % T
                dst = neg_max[unit % 2][:, :].rearrange("p (h t) -> p h t", t=T)
                vec.tensor_reduce(dst[:, 2 * pair:2 * pair + 2, qt], ps_max[r % 2][:, :, :], AX_X, ALU.max,
                                  negate=True).then_inc(row_max, 1)

            def ahead(b, s):
                r = s + LEAD
                if r < SPB:
                    reduce_rows(b, r)
                elif not last(b):
                    reduce_rows(b + 1, r - SPB)

            def body(b, par):
                n, more = b + 1, not last(b)
                for o, c, cpar, s in steps(b, par):
                    if more and o == 2:
                        dve.wait_ge(stats_ready, n + 1)
                    ahead(c, s)
                    if o == 2 and not ended(b):
                        take_ffn_v(b)
                    if not first(b) and not ended(b):
                        if o == 15:
                            invert(b - 1)
                        if o == 20:
                            normalise(b - 1)
                        if o == 28:
                            finish(b - 1, 1 - par)
                    if more:
                        if o == 1:
                            layer_norm_stats(n, 1 - par)
                        if o == 2:
                            mean_variance(n)
                        if o == 4:
                            layer_norm(n, 1 - par)
                        if o == 9:
                            cos_half("k", n)
                        if o == 11:
                            cos_half("q", n)
                        if o == 12:
                            add_linear("k", n)
                        if o == 14:
                            add_linear("q", n)

            vec.memset(half[:, :], -0.5).then_inc(stored, DMA)
            vec.memset(xT[:, 0:1], 0.0).then_inc(edge_filled, 1)
            vec.memset(vals[0][:, :, :, :], 1.0).then_inc(vals_filled, 1)
            layer_norm_stats(0, 0)
            dve.wait_ge(stats_ready, 1)
            mean_variance(0)
            dve.wait_ge(consts_in, CONSTS)
            vec.tensor_scalar(cols[:, OMU_R:OMU_K + 1], cols[:, MU_R:MU_K + 1], -1.0, 1.0,
                              ALU.mult, ALU.add).then_inc(omu_ready, 1)
            vec.tensor_scalar(w_sq[:, FFN_V, :], w_sq[:, FFN_V, :], 0.5, None, ALU.mult).then_inc(halved, 1)
            layer_norm(0, 0)
            dve.wait_ge(trig_in, DMA)
            cos_half("k", 0)
            dve.wait_ge(ready["bias"], 1)
            vec.tensor_tensor(b_fold[:, :].rearrange("p (h k) -> p h k", h=2), ps_bias,
                              cols[:, B_UQ:B_UV + 1].rearrange("p (h k) -> p h k", h=2),
                              ALU.add).then_inc(taken["bias"], 1)
            sin_half(dve, vec, "k", 0)
            dve.wait_ge(taken["bias"], 1)
            vec.tensor_scalar(bv_wide[:, :], w_sq[:, IDENT, :], 0.0, b_fold[:, F_V:F_V + 1],
                              ALU.mult, ALU.add).then_inc(bv_ready, 1)
            add_halves(dve, vec, "k", 0)
            cos_half("q", 0)
            add_linear("k", 0)
            sin_half(dve, vec, "q", 0)
            rest_after_part0(dve, vec, "k", 0)
            add_halves(dve, vec, "q", 0)
            part2(dve, vec, "k", 0)
            add_linear("q", 0)
            rest_after_part0(dve, vec, "q", 0)
            part2(dve, vec, "q", 0)
            dve.wait_ge(ready["row"], 1)
            dve.wait_ge(row_in, DMA)
            vec.tensor_tensor(row_sum[:, :], ps_row, row_o[:, :], ALU.add).then_inc(taken["row"], 1)
            vec.memset(vals[1][:, :, :, :], 1.0).then_inc(vals_filled, 1)
            for r in range(LEAD - STEPS):
                reduce_rows(0, r)
            batches(dve, body)
            invert(B - 1, OTHERS)
            dve.wait_ge(tail_sum_ready, 1)
            normalise_tail(0)
            normalise(B - 1, OTHERS)
            normalise_tail(1)
            finish(B - 1, 1)

        @block.gpsimd
        def _(pool):
            gp = nc.gpsimd

            def inverse_std(n):
                pool.wait_ge(var_ready, n + 1)
                gp.tensor_tensor(rstd[:, :], var_eps[:, :], half[:, :], ALU.pow).then_inc(rstd_ready, 1)

            def split_max(unit, u):
                pool.wait_ge(row_max, STEPS * (unit + 1))
                if not (isinstance(unit, int) and unit == 0):
                    pool.wait_ge(ready["max"], unit)
                src = neg_max[u % 2]
                gp.tensor_tensor(max_parts[:, 0, :], src[:, :], zeros[:, :],
                                 ALU.add).then_inc(max_split, 1)
                pool.wait_ge(max_split, 3 * unit + 1)
                gp.tensor_tensor(max_rest[:, :], src[:, :], max_parts[:, 0, :],
                                 ALU.subtract).then_inc(max_split, 1)
                pool.wait_ge(max_split, 3 * unit + 2)
                gp.tensor_tensor(max_parts[:, 1, :], max_rest[:, :], zeros[:, :],
                                 ALU.add).then_inc(max_split, 1)
                pool.wait_ge(max_split, 3 * unit + 3)
                gp.tensor_tensor(max_parts[:, 2, :], max_rest[:, :], max_parts[:, 1, :],
                                 ALU.subtract).then_inc(max_parts_ready, 1)

            def mix(name, n):
                mu, omu = (MU_R, OMU_R) if name == "r" else (MU_K, OMU_K)
                gp.tensor_scalar(mix_a[name][:, :], xT[:, 1:1 + S], cols[:, mu:mu + 1], 0.0,
                                 ALU.mult, ALU.add)
                gp.tensor_scalar(mix_b[name][:, :], xT[:, 0:S], cols[:, omu:omu + 1], 0.0,
                                 ALU.mult, ALU.add).then_inc(mix_half, 1)
                pool.wait_ge(mix_half, 2 * n + (1 if name == "r" else 2))
                if not (isinstance(n, int) and n == 0):
                    pool.wait_ge(ready[f"ffn_{name}"], n)
                gp.tensor_tensor(mixed[name][:, :], mix_a[name][:, :], mix_b[name][:, :],
                                 ALU.add).then_inc(mixed_ready[name], 1)

            def square(n):
                pool.wait_ge(taken["ffn_k"], n + 1)
                if not (isinstance(n, int) and n == 0):
                    pool.wait_ge(ready["ffn_v"], n)
                gp.tensor_tensor(relu_sq[:, :], relu[:, :], relu[:, :], ALU.mult).then_inc(relu_sq_ready, 1)

            def residual(n, par):
                for t in range(T):
                    last_op = gp.tensor_tensor(x_bias[:, t, :], x_in[par][:, t, :], row_sum[:, :], ALU.add)
                last_op.then_inc(x_bias_ready, 1)

            def add_gated(n, par):
                pool.wait_ge(taken["ffn_v"], n + 1)
                pool.wait_ge(x_bias_ready, n + 1)
                gp.tensor_tensor(base[par][:, :, :], x_bias[:, :, :], gated[:, :, :],
                                 ALU.add).then_inc(base_ready, 1)

            def body(b, par):
                n, more = b + 1, not last(b)
                for o, c, cpar, s in steps(b, par):
                    if o == 2 and more:
                        inverse_std(n)
                    if o % STEPS == 3 and not ended(b):
                        split_max(UNITS * b + o // STEPS, o // STEPS)
                    if o == 4 and not ended(b):
                        add_gated(b, par)
                    if more:
                        if o == 10:
                            sin_half(pool, gp, "k", n)
                            add_halves(pool, gp, "k", n)
                        if o == 12:
                            sin_half(pool, gp, "q", n)
                            add_halves(pool, gp, "q", n)
                        if o == 14:
                            rest_after_part0(pool, gp, "k", n)
                            mix("r", n)
                        if o == 16:
                            part2(pool, gp, "k", n)
                            rest_after_part0(pool, gp, "q", n)
                        if o == 19:
                            part2(pool, gp, "q", n)
                            mix("k", n)
                        if o == 22:
                            residual(n, 1 - par)
                        if o == 25:
                            square(n)

            gp.memset(max_cols[:, :], 0.0)
            gp.memset(zeros[:, :], 0.0).then_inc(cleared, 1)
            gp.memset(q_stack[0][:, :, :].bitcast(F32), 0.0).then_inc(cleared, 1)
            pool.wait_ge(edge_filled, 1)
            inverse_std(0)
            pool.wait_ge(cleared, 2)
            pool.wait_ge(rstd_ready, 1)
            gp.memset(k_stack[0][0:MAX_AT, :, :].bitcast(F32), 0.0).then_inc(cleared, 1)
            pool.wait_ge(cleared, 3)
            gp.memset(k_stack[0][MAX_AT:P, :, :].bitcast(F32), TWO_ONES).then_inc(cleared, 1)
            pool.wait_ge(cleared, 4)
            pool.wait_ge(omu_ready, 1)
            pool.wait_ge(taken["xT"], 1)
            mix("r", 0)
            mix("k", 0)
            square(0)
            pool.wait_ge(taken["row"], 1)
            residual(0, 0)
            gp.memset(q_stack[1][:, :, :].bitcast(F32), 0.0)
            gp.memset(k_stack[1][:, :, :].bitcast(F32), 0.0).then_inc(cleared, 1)
            pool.wait_ge(cleared, 5)
            gp.memset(k_stack[1][MAX_AT:P, :, :].bitcast(F32), TWO_ONES).then_inc(cleared, 1)
            pool.wait_ge(cleared, 6)
            batches(pool, body)


def kernel(**inputs):
    import ml_dtypes
    import concourse.bacc as bacc
    from concourse.bass_utils import run_bass_kernel_spmd

    g = {k[3:]: np.asarray(v) for k, v in inputs.items()}

    def w(name):
        return g[name]

    w_sq = np.stack([
        np.concatenate([w("attn_Wd_q_w"), w("attn_Wd_kv_w")], axis=1).T, w("attn_Wk_r_w"), w("attn_Wo_w"),
        w("ffn_W_r").T, w("ffn_W_k").T, w("ffn_W_v").T, np.eye(D, dtype=np.float32),
    ], axis=1)
    w_lat = np.stack([
        np.concatenate([w("attn_Wu_q_w"), w("attn_Wu_k_w")], axis=0),
        np.concatenate([w("attn_Wq_r_w"), w("attn_Wu_v_w")], axis=0),
    ], axis=1)
    cols = np.stack([
        np.concatenate([w("attn_Wd_q_b"), w("attn_Wd_kv_b")]),
        w("attn_Wk_r_b"), w("attn_Wu_q_b"), w("attn_Wq_r_b"), w("attn_Wu_k_b"), w("attn_Wu_v_b"),
        w("ffn_mu_r"), w("ffn_mu_k"),
    ], axis=1)
    strips = np.arange(P) // VW
    w_out_strips = np.zeros((P, D), np.float32)
    w_out_strips.reshape(HPU, VW, D)[:, 0:HD] = w("attn_Wo_w")[-HPU * HD:].reshape(HPU, HD, D)
    sum_to_strip = (np.arange(P)[:, None] == VW * strips[None, :] + HD).astype(np.float32)
    w_tail = np.stack([w_out_strips, sum_to_strip], axis=1)
    theta = (np.float32(10000.0) ** (np.float32(-2.0) * np.arange(D // 2, dtype=np.float32))
             / np.float32(D // 2)).astype(np.float32)
    angle = (np.arange(S, dtype=np.float32)[None, :] * np.repeat(theta, 2)[:, None]).astype(np.float32)
    sign = np.where(np.arange(D) % 2 == 0, -1.0, 1.0).astype(np.float32)[:, None]
    trig = np.stack([np.cos(angle), np.sin(angle) * sign], axis=1).astype(np.float32)

    arrays = {
        "x_dram": g["attn_x"], "w_sq_dram": w_sq, "w_lat_dram": w_lat, "cols_dram": cols,
        "row_o_dram": np.broadcast_to(w("attn_Wo_b"), (P, D)), "trig_dram": trig,
        "ident_dram": np.eye(P).astype(ml_dtypes.bfloat16),
        "w_tail_dram": w_tail,
    }
    arrays = {k: np.ascontiguousarray(v) for k, v in arrays.items()}
    nc = bacc.Bacc("TRN2", target_bir_lowering=False, num_devices=1)
    args = [nc.dram_tensor(k, v.shape, mybir.dt.from_np(v.dtype), kind="ExternalInput").ap()
            for k, v in arrays.items()]
    out = nc.dram_tensor("out_dram", (B, S, D), F32, kind="ExternalOutput").ap()
    build(nc, *args, out)
    r = run_bass_kernel_spmd(nc, [arrays], core_ids=[0])
    return r.results[0]["out_dram"]
```
